# Optimizing a Trainium2 kernel written in Bass

```python
import numpy as np
import jax
import jax.numpy as jnp

def _softmax(x, axis=-1):
    return jax.nn.softmax(x, axis=axis)

def _gelu(x):
    return jax.nn.gelu(x, approximate=True)

def _silu(x):
    return jax.nn.silu(x)

def _sigmoid(x):
    return jax.nn.sigmoid(x)

def _layernorm(x, axis=-1, eps=1e-05):
    m = jnp.mean(x, axis=axis, keepdims=True)
    v = jnp.var(x, axis=axis, keepdims=True)
    return (x - m) / jnp.sqrt(v + eps)

def _scatter_add(tgt, idx, src, axis=0):
    return tgt.at[idx].add(src)

def _segment_sum(src, seg, n):
    return jax.ops.segment_sum(src, seg, n)
kernel_name = 'mk_cond_seq_d1_seqx_r4_be7537'

def setup_inputs(seed: int=0):
    np.random.seed(seed)
    _w = jnp.asarray

    def _rec_inputs():
        import jax
        import jax.numpy as jnp
        _rk = jax.random.key(seed)
        x = -0.0002928 + 1 * jax.random.normal(jax.random.fold_in(_rk, 1), (32, 64, 256), jnp.float32)
        _lenS = 64 - jax.random.randint(jax.random.fold_in(_rk, 7), (32,), 0, max(1, 64 // 4) + 1, jnp.int32)
        _lenS2 = 64 - jax.random.randint(jax.random.fold_in(_rk, 8), (32,), 0, max(1, 64 // 4) + 1, jnp.int32)
        cond_1024 = 0.000887014 + 1.03683 * jax.random.normal(jax.random.fold_in(_rk, 11), (32, 256), jnp.float32)
        _validS = jnp.arange(64)[None, :] < _lenS[:, None]
        _validS2 = jnp.arange(64)[None, :] < _lenS2[:, None]
        _causal = jnp.tril(jnp.ones((64, 64), dtype=bool))
        mask_BxS_ik0 = jnp.where(jnp.broadcast_to(_validS[:, :], (32, 64)), 0, 1).astype(jnp.int32)
        return (x, cond_1024, mask_BxS_ik0)
    x, cond_1024, mask_BxS_ik0 = _rec_inputs()

    def _L0_cond_setup():
        import jax, jax.numpy as jnp
        import numpy as np
        EMBED = 256
        HEADS = 16
        HEAD_DIM = EMBED // HEADS
        MLP = 4 * EMBED
        EPS = 1e-06

        def _adaln(x, c, norm_w, scale_w, scale_b, shift_w, shift_b):
            sc = jax.nn.silu(c)
            shift = sc @ shift_w.T + shift_b
            scale = jnp.clip(sc @ scale_w.T + scale_b + 1.0, 0.1, 10.0)
            norm = jnp.maximum(jnp.linalg.norm(x, axis=-1, keepdims=True) * x.shape[-1] ** (-0.5), EPS)
            h = x / norm * norm_w
            return h * scale[:, None, :] + shift[:, None, :]

        def _attention(x, attention_mask, qkv_w, proj_w, proj_b):
            B, N, C = x.shape
            qkv = (x @ qkv_w.T).reshape(B, N, 3, HEADS, HEAD_DIM)
            q = qkv[:, :, 0].transpose(0, 2, 1, 3)
            k = qkv[:, :, 1].transpose(0, 2, 1, 3)
            v = qkv[:, :, 2].transpose(0, 2, 1, 3)
            attn = jnp.einsum('bhnd,bhmd->bhnm', q, k) * HEAD_DIM ** (-0.5)
            mask = attention_mask[:, None, None, :]
            attn = jnp.where(mask == 0, -jnp.inf, attn)
            all_inf = jnp.all(attn == -jnp.inf, axis=-1, keepdims=True)
            attn = jnp.where(all_inf, 0.0, attn)
            p = jax.nn.softmax(attn, axis=-1)
            out = jnp.einsum('bhnm,bhmd->bhnd', p, v).transpose(0, 2, 1, 3).reshape(B, N, C)
            return out @ proj_w.T + proj_b

        def _mlp(x, w1, b1, w2, b2):
            h = x @ w1.T + b1
            x1, x2 = jnp.split(h, 2, axis=-1)
            return jax.nn.silu(x1) * x2 @ w2.T + b2
        key = jax.random.key(seed)
        ks = jax.random.split(key, 16)
        B, N, C = (2, 512, EMBED)
        x = jax.random.normal(ks[0], (B, N, C), dtype=jnp.float32)
        c = jax.random.normal(ks[1], (B, C), dtype=jnp.float32)
        attention_mask = jax.random.randint(ks[2], (B, N), 0, 2, dtype=jnp.int32)
        s = 0.02
        params = {'norm_w': jnp.ones((C,), jnp.float32), 'scale_w': s * jax.random.normal(ks[3], (C, C), jnp.float32), 'scale_b': s * jax.random.normal(ks[4], (C,), jnp.float32), 'shift_w': s * jax.random.normal(ks[5], (C, C), jnp.float32), 'shift_b': s * jax.random.normal(ks[6], (C,), jnp.float32), 'qkv_w': s * jax.random.normal(ks[7], (3 * C, C), jnp.float32), 'proj_w': s * jax.random.normal(ks[8], (C, C), jnp.float32), 'proj_b': s * jax.random.normal(ks[9], (C,), jnp.float32), 'mlp_w1': s * jax.random.normal(ks[10], (2 * MLP, C), jnp.float32), 'mlp_b1': s * jax.random.normal(ks[11], (2 * MLP,), jnp.float32), 'mlp_w2': s * jax.random.normal(ks[12], (C, MLP), jnp.float32), 'mlp_b2': s * jax.random.normal(ks[13], (C,), jnp.float32)}
        return {'x': x, 'c': c, 'attention_mask': attention_mask, **params}
    _L0_cond_all = _L0_cond_setup()
    _L0_cond_in = {k: v for k, v in _L0_cond_all.items() if k in ('norm_w', 'scale_w', 'scale_b', 'shift_w', 'shift_b', 'qkv_w', 'proj_w', 'proj_b', 'mlp_w1', 'mlp_b1', 'mlp_w2', 'mlp_b2')}
    del _L0_cond_all
    return {'x': x, 'cond_1024': cond_1024, 'mask_BxS_ik0': mask_BxS_ik0, 'L0_cond_norm_w': _L0_cond_in['norm_w'], 'L0_cond_scale_w': _L0_cond_in['scale_w'], 'L0_cond_scale_b': _L0_cond_in['scale_b'], 'L0_cond_shift_w': _L0_cond_in['shift_w'], 'L0_cond_shift_b': _L0_cond_in['shift_b'], 'L0_cond_qkv_w': _L0_cond_in['qkv_w'], 'L0_cond_proj_w': _L0_cond_in['proj_w'], 'L0_cond_proj_b': _L0_cond_in['proj_b'], 'L0_cond_mlp_w1': _L0_cond_in['mlp_w1'], 'L0_cond_mlp_b1': _L0_cond_in['mlp_b1'], 'L0_cond_mlp_w2': _L0_cond_in['mlp_w2'], 'L0_cond_mlp_b2': _L0_cond_in['mlp_b2']}

def reference(x, cond_1024, mask_BxS_ik0, L0_cond_norm_w, L0_cond_scale_w, L0_cond_scale_b, L0_cond_shift_w, L0_cond_shift_b, L0_cond_qkv_w, L0_cond_proj_w, L0_cond_proj_b, L0_cond_mlp_w1, L0_cond_mlp_b1, L0_cond_mlp_w2, L0_cond_mlp_b2):
    import jax
    import jax.numpy as jnp

    def _L0_cond_ref(x, c, attention_mask, norm_w, scale_w, scale_b, shift_w, shift_b, qkv_w, proj_w, proj_b, mlp_w1, mlp_b1, mlp_w2, mlp_b2):
        import jax, jax.numpy as jnp
        import numpy as np
        EMBED = 256
        HEADS = 16
        HEAD_DIM = EMBED // HEADS
        MLP = 4 * EMBED
        EPS = 1e-06

        def _adaln(x, c, norm_w, scale_w, scale_b, shift_w, shift_b):
            sc = jax.nn.silu(c)
            shift = sc @ shift_w.T + shift_b
            scale = jnp.clip(sc @ scale_w.T + scale_b + 1.0, 0.1, 10.0)
            norm = jnp.maximum(jnp.linalg.norm(x, axis=-1, keepdims=True) * x.shape[-1] ** (-0.5), EPS)
            h = x / norm * norm_w
            return h * scale[:, None, :] + shift[:, None, :]

        def _attention(x, attention_mask, qkv_w, proj_w, proj_b):
            B, N, C = x.shape
            qkv = (x @ qkv_w.T).reshape(B, N, 3, HEADS, HEAD_DIM)
            q = qkv[:, :, 0].transpose(0, 2, 1, 3)
            k = qkv[:, :, 1].transpose(0, 2, 1, 3)
            v = qkv[:, :, 2].transpose(0, 2, 1, 3)
            attn = jnp.einsum('bhnd,bhmd->bhnm', q, k) * HEAD_DIM ** (-0.5)
            mask = attention_mask[:, None, None, :]
            attn = jnp.where(mask == 0, -jnp.inf, attn)
            all_inf = jnp.all(attn == -jnp.inf, axis=-1, keepdims=True)
            attn = jnp.where(all_inf, 0.0, attn)
            p = jax.nn.softmax(attn, axis=-1)
            out = jnp.einsum('bhnm,bhmd->bhnd', p, v).transpose(0, 2, 1, 3).reshape(B, N, C)
            return out @ proj_w.T + proj_b

        def _mlp(x, w1, b1, w2, b2):
            h = x @ w1.T + b1
            x1, x2 = jnp.split(h, 2, axis=-1)
            return jax.nn.silu(x1) * x2 @ w2.T + b2
        x = x + _attention(_adaln(x, c, norm_w, scale_w, scale_b, shift_w, shift_b), attention_mask, qkv_w, proj_w, proj_b)
        x = x + _mlp(_adaln(x, c, norm_w, scale_w, scale_b, shift_w, shift_b), mlp_w1, mlp_b1, mlp_w2, mlp_b2)
        return x
    x = _L0_cond_ref(x, cond_1024, mask_BxS_ik0, L0_cond_norm_w, L0_cond_scale_w, L0_cond_scale_b, L0_cond_shift_w, L0_cond_shift_b, L0_cond_qkv_w, L0_cond_proj_w, L0_cond_proj_b, L0_cond_mlp_w1, L0_cond_mlp_b1, L0_cond_mlp_w2, L0_cond_mlp_b2)
    return x

_drawn_inputs = setup_inputs


def setup_inputs(seed=0):
    import zlib

    import numpy as np

    out = dict(_drawn_inputs(seed))
    spreads = {'L0_cond_norm_w': (1.0, 0.6)}
    factors = {'L0_cond_scale_w': 3.961,
     'L0_cond_scale_b': 22.36,
     'L0_cond_shift_b': 8.0,
     'L0_cond_proj_b': 2.744,
     'L0_cond_mlp_b1': 8.0,
     'L0_cond_mlp_b2': 2.7}
    for name, (base, spread) in spreads.items():
        noise = np.random.default_rng([zlib.crc32(name.encode()), seed]).standard_normal(out[name].shape)
        drawn = base * np.exp(spread * noise) if base else spread * noise
        out[name] = jnp.asarray(drawn.astype(out[name].dtype))
    for name, factor in factors.items():
        out[name] = (out[name] * factor).astype(out[name].dtype)
    return out
```

```python
from contextlib import ExitStack

import concourse.bass as bass
from concourse import mybir

F32 = mybir.dt.float32
F32R = mybir.dt.float32r
BF16 = mybir.dt.bfloat16
F16 = mybir.dt.float16
I32 = mybir.dt.int32
ALU = mybir.AluOpType
ACT = mybir.ActivationFunctionType
AX_X = mybir.AxisListType.X

P = 128
BATCH, SEQ, C = 32, 64, 256
HEADS = 16
D = C // HEADS
F = 4 * C
TILES = 4
GTOK = TILES * P
GROUPS = BATCH * SEQ // GTOK
BT = P // SEQ
BG = TILES * BT
NT = GROUPS * TILES
CK = C // P
HC = HEADS // CK
FJ = F // P
PAIRS = HEADS // 2
SCALE = float(D) ** -0.5
EPS = 1e-6
MASKED = -1.0e30
EXP_SHIFT = 9.7
VW = D + 1

WCH = 1024
QK_AT, V_AT = 0, CK * 2 * C
PR_AT = V_AT + CK * C
W1_AT = PR_AT + CK * C
W2_AT = W1_AT + CK * 2 * F
W_COLS = W2_AT + FJ * C
W_CHUNKS = W_COLS // WCH
SCALE_B, SHIFT_B, NORM_W, MLP_B1 = 0, CK, 2 * CK, 3 * CK
VEC_COLS = 3 * CK + 2 * FJ


def block_kernel(nc, x, cond_t, mask, weights, mod_w, vecs, rows, out):
    x_v = x.rearrange("(g t p) c -> g p t c", g=GROUPS, t=TILES)
    out_v = out.rearrange("(n p) c -> n p c", p=P)

    with ExitStack() as ctx:
        def sb(name, shape, dt=F32):
            return ctx.enter_context(nc.sbuf_tensor(name, shape, dt))

        def ps(name, shape):
            return ctx.enter_context(nc.psum_tensor(name, shape, F32))

        def sem(name):
            return ctx.enter_context(nc.semaphore(name))

        w_hi = sb("w_hi", [P, W_COLS], F32R)
        w_lo = sb("w_lo", [P, W_COLS], F32R)
        w_raw = sb("w_raw", [P, 2, WCH])
        vec = sb("vec", [P, VEC_COLS])
        proj_b = sb("proj_b", [P, C])
        mlp_b2 = sb("mlp_b2", [P, C])
        ident = sb("ident", [P, P])
        head_rows = sb("head_rows", [P, HC])
        exp_shift = sb("exp_shift", [P, 1])
        neg_half = sb("neg_half", [P, TILES])
        cond = sb("cond", [P, CK, BATCH])
        scale_w = sb("scale_w", [P, CK, BATCH])
        shift = sb("shift", [P, CK, BATCH])
        mask_add = sb("mask_add", [P, NT, SEQ])
        all_masked = sb("all_masked", [P, NT])
        score_mul = sb("score_mul", [P, NT])
        x_in = sb("x_in", [P, TILES, C])
        x_nrm = sb("x_nrm", [P, TILES, C])
        x_res = sb("x_res", [P, TILES, C])
        x_ssq = sb("x_ssq", [P, TILES])
        x_pow = sb("x_pow", [P, TILES])
        x_inv = sb("x_inv", [P, TILES])
        x1 = sb("x1", [P, TILES, C])
        x1_nrm = sb("x1_nrm", [P, TILES, C])
        x1_ssq = sb("x1_ssq", [P, TILES])
        x1_pow = sb("x1_pow", [P, TILES])
        x1_inv = sb("x1_inv", [P, TILES])
        y = sb("y", [P, TILES, C])
        h_full = sb("h_full", [P, CK, GTOK])
        h1_hi = sb("h1_hi", [P, CK, GTOK], F32R)
        h1_lo = sb("h1_lo", [P, CK, GTOK], F32R)
        h2_hi = sb("h2_hi", [P, CK, GTOK], F32R)
        h2_lo = sb("h2_lo", [P, CK, GTOK], F32R)
        q_t = sb("q_t", [P, CK, GTOK])
        k_t = sb("k_t", [P, CK, GTOK])
        k_diag = sb("k_diag", [P, 2, CK, BT, HC * SEQ])
        s_sb = sb("s_sb", [P, 2, HEADS * SEQ])
        s_max = sb("s_max", [P, 2, HEADS])
        p_hi = sb("p_hi", [P, PAIRS, P], F16)
        p_lo = sb("p_lo", [P, PAIRS, P], F16)
        v_part = sb("v_part", [P, 3, PAIRS, 2, D], BF16)
        v_rest = sb("v_rest", [P, C])
        v_diag = sb("v_diag", [P, 2, PAIRS, 3, BT, 2, VW], BF16)
        sum_inv = sb("sum_inv", [P, 2, HC])
        o_sb = sb("o_sb", [P, C])
        o_hi = sb("o_hi", [P, C], F32R)
        o_lo = sb("o_lo", [P, C], F32R)
        gate = sb("gate", [P, 2, GTOK])
        g_hi = sb("g_hi", [P, FJ, GTOK], F32R)
        g_lo = sb("g_lo", [P, FJ, GTOK], F32R)
        mask_raw = s_sb[:, 0, :].bitcast(I32).rearrange("p (n k) -> p n k", k=SEQ)
        mod_sb = s_sb[:, 1, :].rearrange("p (s k n) -> p s k n", s=2, k=CK)

        ps_s = ps("ps_s", [P, 2, 512])
        ps_p = ps("ps_p", [P, 2, 512])
        ps_c = ps("ps_c", [P, 2, 512])
        ps_m = ps("ps_m", [P, 2, 512])

        wqk = [w[:, QK_AT:V_AT].rearrange("p (k n) -> p k n", k=CK) for w in (w_hi, w_lo)]
        wv = [w[:, V_AT:PR_AT].rearrange("p (k n) -> p k n", k=CK) for w in (w_hi, w_lo)]
        wpr = [w[:, PR_AT:W1_AT].rearrange("p (k n) -> p k n", k=CK) for w in (w_hi, w_lo)]
        w1 = [w[:, W1_AT:W2_AT].rearrange("p (k n) -> p k n", k=CK) for w in (w_hi, w_lo)]
        w2 = [w[:, W2_AT:W_COLS].rearrange("p (j n) -> p j n", j=FJ) for w in (w_hi, w_lo)]
        h1, h2, o_t, g_t = (h1_hi, h1_lo), (h2_hi, h2_lo), (o_hi, o_lo), (g_hi, g_lo)
        PARTS = ((0, 0), (0, 1), (1, 0))

        vec_loaded, rows_loaded, cond_loaded = sem("vec_loaded"), sem("rows_loaded"), sem("cond_loaded")
        mask_loaded, mod_loaded = sem("mask_loaded"), sem("mod_loaded")
        w_loaded = [sem("w_loaded_even"), sem("w_loaded_odd")]
        w_hi_done, w_lo_done = sem("w_hi_done"), sem("w_lo_done")
        ident_ready, consts_ready = sem("ident_ready"), sem("consts_ready")
        vdiag_ready, mask_step, mod_step = sem("vdiag_ready"), sem("mask_step"), sem("mod_step")
        cond_silu, mod_done, heads_ready = sem("cond_silu"), sem("mod_done"), sem("heads_ready")
        x_loaded, x_squared, x_powed = sem("x_loaded"), sem("x_squared"), sem("x_powed")
        x_inverted, x_normed, x_biased = sem("x_inverted"), sem("x_normed"), sem("x_biased")
        xt_done, h1_scaled, h1_full = sem("xt_done"), sem("h1_scaled"), sem("h1_full")
        h1_hi_done, h1_lo_done = sem("h1_hi_done"), sem("h1_lo_done")
        k_done, k_copied, q_done, q_copied = sem("k_done"), sem("k_copied"), sem("q_done"), sem("q_copied")
        kdiag_built, s_done, s_masked = sem("kdiag_built"), sem("s_done"), sem("s_masked")
        max_done, max_subtracted, exp_done = sem("max_done"), sem("max_subtracted"), sem("exp_done")
        pt_done, p_hi_done, p_lo_done = sem("pt_done"), sem("p_hi_done"), sem("p_lo_done")
        v_done, v1_done, v_rest_done = sem("v_done"), sem("v1_done"), sem("v_rest_done")
        v2_done, v3_done, vdiag_built = sem("v2_done"), sem("v3_done"), sem("vdiag_built")
        pv_done, sum_inverted, o_done = sem("pv_done"), sem("sum_inverted"), sem("o_done")
        ot_done, o_hi_done, o_lo_done = sem("ot_done"), sem("o_hi_done"), sem("o_lo_done")
        proj_done, x1_done = sem("proj_done"), sem("x1_done")
        x1_squared, x1_powed, x1_inverted = sem("x1_squared"), sem("x1_powed"), sem("x1_inverted")
        x1_normed, y_biased = sem("x1_normed"), sem("y_biased")
        x1t_done, h2_scaled, h2_full = sem("x1t_done"), sem("h2_scaled"), sem("h2_full")
        h2_hi_done, h2_lo_done = sem("h2_hi_done"), sem("h2_lo_done")
        gate_done, up_done, silu_done = sem("gate_done"), sem("up_done"), sem("silu_done")
        g_done, g_hi_done, g_lo_done = sem("g_done"), sem("g_hi_done"), sem("g_lo_done")
        down_done = sem("down_done")
        ps_m_read = sem("ps_m_read")
        y_free = sem("y_free")

        block = ctx.enter_context(nc.Block())
        is0 = lambda g: isinstance(g, int) and g == 0

        @block.sync
        def _(sp):
            sp.dma_start(vec[:], vecs).then_inc(vec_loaded, 16)
            sp.dma_start(cond[:], cond_t).then_inc(cond_loaded, 16)

            def load_x(g):
                if not is0(g):
                    sp.wait_ge(x_normed, TILES * g)
                    sp.wait_ge(x_biased, TILES * g)
                src = x_v[g] if isinstance(g, int) else x_v[bass.ds(g, 1)].rearrange("a p t c -> (a p) t c")
                sp.dma_start(x_in[:], src).then_inc(x_loaded, 16)

            def load_w(s):
                if s >= 2:
                    sp.wait_ge(w_hi_done, s - 1)
                    sp.wait_ge(w_lo_done, s - 1)
                sp.dma_start(w_raw[:, s % 2, :], weights[:, s * WCH:(s + 1) * WCH]).then_inc(w_loaded[s % 2], 16)

            load_x(0)
            load_w(0)
            sp.dma_start(proj_b[:], rows[0:1, :].broadcast_to([P, C])).then_inc(rows_loaded, 16)
            sp.dma_start(mlp_b2[:], rows[1:2, :].broadcast_to([P, C])).then_inc(y_free, 16)
            for s in range(1, W_CHUNKS):
                load_w(s)
            load_x(1)

            def store_y(g):
                for t in range(TILES):
                    n = TILES * g + t
                    sp.wait_ge(ps_m_read, n + 2)
                    dst = out_v[n] if isinstance(n, int) else out_v[bass.ds(n, 1)].rearrange("a p c -> (a p) c")
                    sp.dma_start(dst, y[:, t, :]).then_inc(y_free, 16)

            with sp.Fori(1, GROUPS - 1) as g:
                load_x(g + 1)
                store_y(g - 1)
            store_y(GROUPS - 2)
            store_y(GROUPS - 1)
            sp.wait_ge(y_free, 16 * NT + 16)

        @block.tensor
        def _(pe):
            def product(dst, lhs, rhs, lhs_at, rhs_at, n):
                for k in range(n):
                    for a, b in PARTS:
                        last = pe.matmul(dst, lhs[a][:, k, lhs_at], rhs[b][:, k, rhs_at],
                                         start=(k == 0 and (a, b) == PARTS[0]),
                                         stop=(k == n - 1 and (a, b) == PARTS[-1]))
                return last

            def modulation():
                pe.wait_ge(cond_silu, 1)
                pe.wait_ge(mod_loaded, 16)
                for s in range(2):
                    for m in range(CK):
                        for k in range(CK):
                            last = pe.matmul(ps_m[:, s, m * BATCH:(m + 1) * BATCH],
                                             mod_sb[:, s, k, m * P:(m + 1) * P], cond[:, k, :],
                                             start=(k == 0), stop=(k == CK - 1))
                    last.then_inc(mod_done, 1)

            def x_transposed(g):
                pe.wait_ge(x_normed, TILES * g + TILES)
                for c in range(CK):
                    if not is0(g):
                        pe.wait_ge(p_lo_done, 2 * TILES * g)
                    for t in range(TILES):
                        last = pe.transpose(ps_p[:, c, t * P:(t + 1) * P], x_nrm[:, t, c * P:(c + 1) * P], ident[:])
                    last.then_inc(xt_done, 1)

            def k_proj(g):
                pe.wait_ge(h1_lo_done, CK * g + CK)
                for c in range(CK):
                    if not is0(g):
                        pe.wait_ge(s_masked, 2 * TILES * g - 1 + c)
                    product(ps_s[:, c, :], wqk, h1, slice(C + c * P, C + (c + 1) * P), slice(0, GTOK), CK)\
                        .then_inc(k_done, 1)

            def q_proj(g):
                for c in range(CK):
                    pe.wait_ge(k_copied, CK * g + c + 1)
                    product(ps_s[:, c, :], wqk, h1, slice(c * P, (c + 1) * P), slice(0, GTOK), CK)\
                        .then_inc(q_done, 1)

            def v_proj(g, t):
                n = TILES * g + t
                if t == 0:
                    pe.wait_ge(h1_scaled, CK * g + CK)
                elif t == 1:
                    pe.wait_ge(v_rest_done, n)
                else:
                    pe.wait_ge(p_lo_done, 2 * (n - 2) + 1)
                product(ps_p[:, 0, 0:C], h1, wv, slice(t * P, (t + 1) * P), slice(0, C), CK).then_inc(v_done, 1)

            def scores(g, t):
                n = TILES * g + t
                pe.wait_ge(kdiag_built, n + 1)
                pe.wait_ge(q_copied, CK * g + CK)
                for c in range(CK):
                    if t > 0:
                        pe.wait_ge(s_masked, 2 * n - 1 + c)
                    for b in range(BT):
                        last = pe.matmul(ps_s[b * SEQ:(b + 1) * SEQ, c, :],
                                         q_t[:, c, t * P + b * SEQ:t * P + (b + 1) * SEQ],
                                         k_diag[:, t % 2, c, b, :], start=True, stop=True)
                    last.then_inc(s_done, 1)

            def p_transposed(g, t):
                n = TILES * g + t
                pe.wait_ge(exp_done, n + 1)
                pe.wait_ge(v_rest_done, TILES * g + min(t + 2, TILES))
                if t > 0:
                    pe.wait_ge(p_lo_done, 2 * n)
                for half in range(2):
                    for j in range(4):
                        at = (half * 4 + j) * P
                        last = pe.transpose(ps_p[:, half, j * P:(j + 1) * P], s_sb[:, t % 2, at:at + P], ident[:])
                    last.then_inc(pt_done, 1)

            def p_times_v(g, t):
                n = TILES * g + t
                pe.wait_ge(vdiag_built, 4 * n + 4)
                if t > 0:
                    pe.wait_ge(o_lo_done, n)
                    pe.wait_ge(x1_done, n)
                elif not is0(g):
                    pe.wait_ge(h2_scaled, CK * g)
                for half in range(2):
                    pe.wait_ge(p_lo_done, 2 * n + half + 1)
                    for j in range(4):
                        pair = half * 4 + j
                        dst = ps_c[:, half, 0:BT * 4 * 2 * VW]\
                            .rearrange("p (b j n) -> p b j n", b=BT, j=4)[:, :, j, :]
                        terms = [(p_hi, 0), (p_hi, 1), (p_hi, 2), (p_lo, 0), (p_lo, 1)]
                        for i, (part, v) in enumerate(terms):
                            last = pe.matmul(dst, part[:, pair, :],
                                             v_diag[:, t % 2, pair, v].rearrange("p b h n -> p b (h n)"),
                                             start=(i == 0), stop=(i == len(terms) - 1))
                last.then_inc(pv_done, 1)

            def o_transposed(g, t):
                pe.wait_ge(o_done, 2 * (TILES * g + t) + 2)
                for c in range(CK):
                    last = pe.transpose(ps_c[:, 0, c * P:(c + 1) * P], o_sb[:, c * P:(c + 1) * P], ident[:])
                last.then_inc(ot_done, 1)

            def projection(g, t):
                pe.wait_ge(o_lo_done, TILES * g + t + 1)
                o_v = [o[:, :].rearrange("p (k n) -> p k n", k=CK) for o in o_t]
                product(ps_c[:, 1, 0:C], o_v, wpr, slice(0, P), slice(0, C), CK).then_inc(proj_done, 1)

            def x1_transposed(g):
                pe.wait_ge(x1_normed, TILES * g + TILES)
                pe.wait_ge(o_lo_done, TILES * g + TILES)
                pe.wait_ge(x1_done, TILES * g + TILES)
                for c in range(CK):
                    for t in range(TILES):
                        last = pe.transpose(ps_c[:, c, t * P:(t + 1) * P], x1_nrm[:, t, c * P:(c + 1) * P], ident[:])
                    last.then_inc(x1t_done, 1)

            def mlp_gate(m, j):
                n = FJ * m + j
                if j == 0:
                    pe.wait_ge(h2_lo_done, CK * m + CK)
                    pe.wait_ge(ps_m_read, TILES * m + 1)
                else:
                    pe.wait_ge(silu_done, n)
                product(ps_m[:, 0, :], w1, h2, slice(j * P, (j + 1) * P), slice(0, GTOK), CK).then_inc(gate_done, 1)

            def mlp_up(m, j):
                n = FJ * m + j
                if j > 0:
                    pe.wait_ge(g_done, n)
                product(ps_m[:, 1, :], w1, h2, slice(F + j * P, F + (j + 1) * P), slice(0, GTOK), CK)\
                    .then_inc(up_done, 1)

            def mlp_down(m, t):
                n = TILES * m + t
                if t == 0:
                    pe.wait_ge(g_lo_done, FJ * m + FJ)
                elif t >= 2:
                    pe.wait_ge(ps_m_read, n)
                product(ps_m[:, t % 2, 0:C], g_t, w2, slice(t * P, (t + 1) * P), slice(0, C), FJ)\
                    .then_inc(down_done, 1)

            def stage_x(g, m):
                for t in range(TILES):
                    if m is not None:
                        mlp_gate(m, 2 * t)
                    p_transposed(g, t)
                    if m is not None:
                        mlp_up(m, 2 * t)
                        mlp_gate(m, 2 * t + 1)
                    p_times_v(g, t)
                    if m is not None:
                        mlp_up(m, 2 * t + 1)
                    o_transposed(g, t)
                    if t + 2 < TILES:
                        v_proj(g, t + 2)
                        scores(g, t + 2)
                    projection(g, t)

            def stage_y(g, m, more):
                if more:
                    x_transposed(g + 1)
                if m is not None:
                    mlp_down(m, 0)
                    mlp_down(m, 1)
                if more:
                    k_proj(g + 1)
                x1_transposed(g)
                if more:
                    q_proj(g + 1)
                if m is not None:
                    mlp_down(m, 2)
                if more:
                    v_proj(g + 1, 0)
                    scores(g + 1, 0)
                if m is not None:
                    mlp_down(m, 3)
                if more:
                    v_proj(g + 1, 1)
                    scores(g + 1, 1)

            pe.wait_ge(ident_ready, 2)
            modulation()
            x_transposed(0)
            pe.wait_ge(w_lo_done, 2)
            k_proj(0)
            q_proj(0)
            for t in range(2):
                v_proj(0, t)
                scores(0, t)
            pe.wait_ge(vdiag_ready, 1)
            stage_x(0, None)
            stage_y(0, None, True)
            pe.wait_ge(w_lo_done, W_CHUNKS)
            with pe.Fori(1, GROUPS - 1) as g:
                stage_x(g, g - 1)
                stage_y(g, g - 1, True)
            last = GROUPS - 1
            stage_x(last, last - 1)
            stage_y(last, last - 1, False)
            for j in range(FJ):
                mlp_gate(last, j)
                mlp_up(last, j)
            for t in range(TILES):
                mlp_down(last, t)

        @block.scalar
        def _(act):
            act.dma_start(mod_sb, mod_w).then_inc(mod_loaded, 16)
            for b in range(BT):
                src = mask.rearrange("(n b) k -> b n k", b=BT)[b:b + 1].broadcast_to([SEQ, NT, SEQ])
                act.dma_start(mask_raw[b * SEQ:(b + 1) * SEQ], src).then_inc(mask_loaded, 16)
            act.wait_ge(cond_loaded, 16)
            act.activation(cond[:], cond[:], ACT.Silu).then_inc(cond_silu, 1)

            def w_split_hi(s):
                act.wait_ge(w_loaded[s % 2], 16 * (s // 2 + 1))
                act.activation(w_hi[:, s * WCH:(s + 1) * WCH], w_raw[:, s % 2, :], ACT.Copy).then_inc(w_hi_done, 1)

            def x_squares(g):
                act.wait_ge(x_loaded, 16 * g + 16)
                if not is0(g):
                    act.wait_ge(xt_done, CK * g)
                    act.wait_ge(x_inverted, g)
                for t in range(TILES):
                    act.activation(x_nrm[:, t, :], x_in[:, t, :], ACT.Square, scale=1.0 / 16.0,
                                   accum_out=x_ssq[:, t:t + 1]).then_inc(x_squared, 1)

            def x_norms(g):
                act.wait_ge(x_inverted, g + 1)
                act.wait_ge(x_squared, TILES * g + TILES)
                for t in range(TILES):
                    act.activation(x_nrm[:, t, :], x_in[:, t, :], ACT.Copy, scale=x_inv[:, t:t + 1])\
                        .then_inc(x_normed, 1)

            def h1_parts(g):
                if not is0(g):
                    act.wait_ge(v_done, TILES * g)
                for c in range(CK):
                    act.wait_ge(h1_full, CK * g + c + 1)
                    act.activation(h1_hi[:, c, :], h_full[:, c, :], ACT.Copy).then_inc(h1_hi_done, 1)

            def h2_parts(g):
                if not is0(g):
                    act.wait_ge(up_done, FJ * g)
                for c in range(CK):
                    act.wait_ge(h2_full, CK * g + c + 1)
                    act.activation(h2_hi[:, c, :], h_full[:, c, :], ACT.Copy).then_inc(h2_hi_done, 1)

            def k_copy(g):
                if not is0(g):
                    act.wait_ge(kdiag_built, TILES * g)
                for c in range(CK):
                    act.wait_ge(k_done, CK * g + c + 1)
                    act.activation(k_t[:, c, :], ps_s[:, c, :], ACT.Copy).then_inc(k_copied, 1)

            def q_copy(g):
                if not is0(g):
                    act.wait_ge(s_done, 2 * TILES * g)
                for c in range(CK):
                    act.wait_ge(q_done, CK * g + c + 1)
                    act.activation(q_t[:, c, :], ps_s[:, c, :], ACT.Copy).then_inc(q_copied, 1)

            def v_first(g, t):
                n = TILES * g + t
                act.wait_ge(v_done, n + 1)
                if not is0(n):
                    act.wait_ge(vdiag_built, 4 * n)
                act.activation(v_part[:, 0].rearrange("p j h d -> p (j h d)"), ps_p[:, 0, 0:C], ACT.Copy)\
                    .then_inc(v1_done, 1)

            def exps(g, t):
                n = TILES * g + t
                act.wait_ge(max_subtracted, n + 1)
                act.activation(s_sb[:, t % 2, :], s_sb[:, t % 2, :], ACT.Exp, bias=exp_shift[:, 0:1])\
                    .then_inc(exp_done, 1)

            def p_first(g, t):
                n = TILES * g + t
                if not is0(n):
                    act.wait_ge(pv_done, n)
                for half in range(2):
                    act.wait_ge(pt_done, 2 * n + half + 1)
                    act.activation(p_hi[:, half * 4:half * 4 + 4, :].rearrange("p j q -> p (j q)"),
                                   ps_p[:, half, :], ACT.Copy).then_inc(p_hi_done, 1)

            def o_first(g, t):
                n = TILES * g + t
                act.wait_ge(ot_done, n + 1)
                if not is0(n):
                    act.wait_ge(proj_done, n)
                act.activation(o_hi[:], ps_c[:, 0, 0:C], ACT.Copy).then_inc(o_hi_done, 1)

            def x1_squares(g, t):
                n = TILES * g + t
                act.wait_ge(x1_done, n + 1)
                if not is0(g):
                    act.wait_ge(x1t_done, CK * g)
                act.activation(x1_nrm[:, t, :], x1[:, t, :], ACT.Square, scale=1.0 / 16.0,
                               accum_out=x1_ssq[:, t:t + 1]).then_inc(x1_squared, 1)

            def silu(m, j):
                n = FJ * m + j
                act.wait_ge(gate_done, n + 1)
                if j >= 2:
                    act.wait_ge(g_lo_done, n - 1)
                act.activation(gate[:, j % 2, :], ps_m[:, 0, :], ACT.Silu,
                               bias=vec[:, MLP_B1 + j:MLP_B1 + j + 1]).then_inc(silu_done, 1)

            def g_first(m, j):
                n = FJ * m + j
                act.wait_ge(g_done, n + 1)
                act.activation(g_hi[:, j, :], gate[:, j % 2, :], ACT.Copy).then_inc(g_hi_done, 1)

            def stage_x(g, m, more):
                for t in range(TILES):
                    if m is not None:
                        silu(m, 2 * t)
                    p_first(g, t)
                    if m is not None:
                        g_first(m, 2 * t)
                        silu(m, 2 * t + 1)
                    if more and t == 2:
                        x_squares(g + 1)
                    if more and t == 3:
                        x_norms(g + 1)
                    if m is not None:
                        g_first(m, 2 * t + 1)
                    if t + 1 < TILES:
                        exps(g, t + 1)
                    o_first(g, t)
                    if t + 2 < TILES:
                        v_first(g, t + 2)
                    x1_squares(g, t)
                    if m is None:
                        for s in range(2 + 2 * t, min(4 + 2 * t, W_CHUNKS)):
                            w_split_hi(s)

            def stage_y(g, more):
                if more:
                    h1_parts(g + 1)
                    k_copy(g + 1)
                    q_copy(g + 1)
                    h2_parts(g)
                    v_first(g + 1, 0)
                    exps(g + 1, 0)
                    v_first(g + 1, 1)
                else:
                    h2_parts(g)

            x_squares(0)
            x_norms(0)
            w_split_hi(0)
            w_split_hi(1)
            h1_parts(0)
            k_copy(0)
            q_copy(0)
            v_first(0, 0)
            act.wait_ge(consts_ready, 2)
            exps(0, 0)
            v_first(0, 1)
            stage_x(0, None, True)
            stage_y(0, True)
            with act.Fori(1, GROUPS - 1) as g:
                stage_x(g, g - 1, True)
                stage_y(g, True)
            last = GROUPS - 1
            stage_x(last, last - 1, False)
            stage_y(last, False)
            for j in range(FJ):
                silu(last, j)
                g_first(last, j)

        @block.gpsimd
        def _(pool):
            pool.memset(ident[:], 0.0).then_inc(ident_ready, 1)
            pool.memset(neg_half[:], -0.5).then_inc(consts_ready, 1)
            pool.memset(exp_shift[:], EXP_SHIFT).then_inc(consts_ready, 1)
            pool.wait_ge(ident_ready, 1)
            pool.affine_select(out=ident[:], in_=ident[:], compare_op=ALU.not_equal, fill=1.0, base=0,
                               pattern=[[-1, P]], channel_multiplier=1).then_inc(ident_ready, 1)

            def x_inverse(g):
                if not is0(g):
                    pool.wait_ge(x_inverted, g)
                pool.wait_ge(x_squared, TILES * g + TILES)
                pool.tensor_tensor(x_pow[:], x_ssq[:], neg_half[:], ALU.pow).then_inc(x_powed, 1)

            def x_bias(g):
                pool.wait_ge(x_loaded, 16 * g + 16)
                if not is0(g):
                    pool.wait_ge(x1_done, TILES * g)
                for t in range(TILES):
                    pool.tensor_tensor(x_res[:, t, :], x_in[:, t, :], proj_b[:], ALU.add).then_inc(x_biased, 1)

            def k_diagonal(g, t):
                n = TILES * g + t
                pool.wait_ge(k_copied, CK * g + CK)
                if isinstance(n, int) and n < 2:
                    pass
                else:
                    pool.wait_ge(s_done, 2 * n - 2)
                for c in range(CK):
                    dst = k_diag[:, t % 2, c].rearrange("p b (h k) -> p b h k", h=HC)
                    src = k_t[:, c, t * P:(t + 1) * P].rearrange("p (b k) -> p b k", b=BT)\
                        .unsqueeze(2).broadcast_to([P, BT, HC, SEQ])
                    of_head = head_rows[:].unsqueeze(1).unsqueeze(3).broadcast_to([P, BT, HC, SEQ])
                    last = pool.tensor_tensor(dst, src, of_head, ALU.mult)
                last.then_inc(kdiag_built, 1)

            def subtract_max(g, t):
                n = TILES * g + t
                pool.wait_ge(max_done, n + 1)
                s_v = s_sb[:, t % 2, :].rearrange("p (h k) -> p h k", h=HEADS)
                pool.tensor_tensor(s_v, s_v, s_max[:, t % 2, :].unsqueeze(2).broadcast_to([P, HEADS, SEQ]),
                                   ALU.subtract).then_inc(max_subtracted, 1)

            def x1_inverse(g, t):
                n = TILES * g + t
                pool.wait_ge(x1_squared, n + 1)
                if not is0(g):
                    pool.wait_ge(x1_inverted, n - TILES + 1)
                pool.tensor_tensor(x1_pow[:, t:t + 1], x1_ssq[:, t:t + 1], neg_half[:, t:t + 1], ALU.pow)\
                    .then_inc(x1_powed, 1)

            def y_bias(g, t):
                n = TILES * g + t
                pool.wait_ge(x1_done, n + 1)
                pool.wait_ge(y_free, 16 * TILES * g + 16)
                pool.tensor_tensor(y[:, t, :], x1[:, t, :], mlp_b2[:], ALU.add).then_inc(y_biased, 1)

            def stage_x(g, more):
                for t in range(TILES):
                    if more and t == 3:
                        x_inverse(g + 1)
                    if t + 1 < TILES:
                        subtract_max(g, t + 1)
                    if t > 0:
                        x1_inverse(g, t - 1)
                    if not is0(g):
                        y_bias(g - 1, t)
                    if t + 2 < TILES:
                        k_diagonal(g, t + 2)
                x1_inverse(g, TILES - 1)

            def stage_y(g, more):
                if more:
                    k_diagonal(g + 1, 0)
                    k_diagonal(g + 1, 1)
                    x_bias(g + 1)
                    subtract_max(g + 1, 0)

            pool.wait_ge(consts_ready, 1)
            x_inverse(0)
            pool.wait_ge(heads_ready, 1)
            k_diagonal(0, 0)
            k_diagonal(0, 1)
            pool.wait_ge(rows_loaded, 16)
            x_bias(0)
            subtract_max(0, 0)
            stage_x(0, True)
            stage_y(0, True)
            with pool.Fori(1, GROUPS - 1) as g:
                stage_x(g, True)
                stage_y(g, True)
            last = GROUPS - 1
            stage_x(last, False)
            for t in range(TILES):
                y_bias(last, t)

        @block.vector
        def _(dve):
            dve.memset(v_diag[:], 0.0).then_inc(mask_step, 1)
            dve.wait_ge(ident_ready, 2)
            dve.tensor_reduce(head_rows[:], ident[:].rearrange("p (h d) -> p h d", d=D), AX_X, ALU.add)\
                .then_inc(heads_ready, 1)
            dve.wait_ge(mask_step, 1)
            for hp in range(2):
                for b in range(BT):
                    last = dve.memset(v_diag[hp * SEQ:(hp + 1) * SEQ, :, :, 0, b, hp, D], 1.0)
            last.then_inc(vdiag_ready, 1)
            dve.wait_ge(mask_loaded, 16 * BT)
            dve.tensor_scalar(mask_add[:], mask_raw, 0, None, ALU.is_equal).then_inc(mask_step, 1)
            dve.wait_ge(mask_step, 2)
            dve.tensor_reduce(all_masked[:], mask_add[:], AX_X, ALU.min).then_inc(mask_step, 1)
            dve.wait_ge(mask_step, 3)
            dve.tensor_scalar(score_mul[:], all_masked[:], -SCALE, SCALE, ALU.mult, ALU.add).then_inc(mask_step, 1)
            dve.tensor_tensor(mask_add[:], mask_add[:], all_masked[:].unsqueeze(2).broadcast_to([P, NT, SEQ]),
                              ALU.subtract).then_inc(mask_step, 1)
            dve.wait_ge(mask_step, 5)
            dve.tensor_scalar(mask_add[:], mask_add[:], MASKED, None, ALU.mult).then_inc(mask_step, 1)

            def w_split_lo(s):
                dve.wait_ge(w_hi_done, s + 1)
                cols = slice(s * WCH, (s + 1) * WCH)
                dve.tensor_tensor(w_lo[:, cols], w_raw[:, s % 2, :], w_hi[:, cols].bitcast(F32), ALU.subtract)\
                    .then_inc(w_lo_done, 1)

            def modulation():
                dve.wait_ge(vec_loaded, 16)
                dve.wait_ge(mod_done, 2)
                for m in range(CK):
                    cols = slice(m * BATCH, (m + 1) * BATCH)
                    dve.tensor_scalar(scale_w[:, m, :], ps_m[:, 0, cols], vec[:, SCALE_B + m:SCALE_B + m + 1], 1.0,
                                      ALU.add, ALU.add).then_inc(mod_step, 1)
                    dve.tensor_scalar(shift[:, m, :], ps_m[:, 1, cols], vec[:, SHIFT_B + m:SHIFT_B + m + 1], None,
                                      ALU.add).then_inc(mod_step, 1)
                dve.wait_ge(mod_step, 2 * CK)
                dve.tensor_scalar(scale_w[:], scale_w[:], 0.1, 10.0, ALU.max, ALU.min).then_inc(mod_step, 1)
                dve.wait_ge(mod_step, 2 * CK + 1)
                for m in range(CK):
                    dve.tensor_scalar(scale_w[:, m, :], scale_w[:, m, :], vec[:, NORM_W + m:NORM_W + m + 1], None,
                                      ALU.mult).then_inc(ps_m_read if m == 0 else mod_step, 1)
                dve.wait_ge(ps_m_read, 1)
                dve.wait_ge(mod_step, 2 * CK + 2)

            def by_seq(table, g, c):
                return table[:, c, bass.ds(BG * g, BG)].unsqueeze(2).broadcast_to([P, BG, SEQ])

            def adaln(g, src, src_done, scaled, full, hi, hi_done, lo, lo_done):
                seqs = lambda ap: ap.rearrange("p (b k) -> p b k", b=BG)
                for c in range(CK):
                    dve.wait_ge(src_done, CK * g + c + 1)
                    dve.tensor_tensor(seqs(h_full[:, c, :]), seqs(src[:, c, :]), by_seq(scale_w, g, c), ALU.mult)\
                        .then_inc(scaled, 1)
                for c in range(CK):
                    dve.wait_ge(scaled, CK * g + c + 1)
                    dve.tensor_tensor(seqs(h_full[:, c, :]), seqs(h_full[:, c, :]), by_seq(shift, g, c), ALU.add)\
                        .then_inc(full, 1)
                for c in range(CK):
                    dve.wait_ge(hi_done, CK * g + c + 1)
                    dve.tensor_tensor(lo[:, c, :], h_full[:, c, :], hi[:, c, :].bitcast(F32), ALU.subtract)\
                        .then_inc(lo_done, 1)

            def adaln1(g):
                if isinstance(g, int) and g < 2:
                    pass
                else:
                    dve.wait_ge(h2_lo_done, CK * (g - 1))
                adaln(g, ps_p, xt_done, h1_scaled, h1_full, h1_hi, h1_hi_done, h1_lo, h1_lo_done)

            def adaln2(g, more):
                if more:
                    dve.wait_ge(h1_lo_done, CK * (g + 2))
                adaln(g, ps_c, x1t_done, h2_scaled, h2_full, h2_hi, h2_hi_done, h2_lo, h2_lo_done)

            def v_rests(g, t):
                n = TILES * g + t
                flat = lambda i: v_part[:, i].rearrange("p j h d -> p (j h d)")
                dve.wait_ge(v1_done, n + 1)
                if not is0(n):
                    dve.wait_ge(v3_done, n)
                dve.tensor_tensor(v_rest[:], ps_p[:, 0, 0:C], flat(0), ALU.subtract).then_inc(v_rest_done, 1)
                dve.wait_ge(v_rest_done, n + 1)
                dve.tensor_copy(flat(1), v_rest[:]).then_inc(v2_done, 1)
                dve.wait_ge(v2_done, n + 1)
                dve.tensor_tensor(flat(2), v_rest[:], flat(1), ALU.subtract).then_inc(v3_done, 1)
                dve.wait_ge(v3_done, n + 1)
                if isinstance(n, int) and n < 2:
                    pass
                else:
                    dve.wait_ge(pv_done, n - 1)
                for b in range(BT):
                    for hp in range(2):
                        dve.tensor_copy(v_diag[hp * SEQ:(hp + 1) * SEQ, t % 2, :, :, b, hp, 0:D],
                                        v_part[b * SEQ:(b + 1) * SEQ, :, :, hp, :].rearrange("p i j d -> p j i d"))\
                            .then_inc(vdiag_built, 1)

            def mask_and_max(g, t):
                n = TILES * g + t
                if isinstance(n, int) and n < 2:
                    pass
                else:
                    dve.wait_ge(pt_done, 2 * n - 2)
                heads = lambda ap: ap.rearrange("p (h k) -> p h k", k=SEQ)
                for c in range(CK):
                    dve.wait_ge(s_done, 2 * n + c + 1)
                    dve.scalar_tensor_tensor(out=heads(s_sb[:, t % 2, c * 512:(c + 1) * 512]),
                                             in0=heads(ps_s[:, c, :]), scalar=score_mul[:, bass.ds(n, 1)],
                                             in1=mask_add[:, bass.ds(n, 1), :].broadcast_to([P, HC, SEQ]),
                                             op0=ALU.mult, op1=ALU.add).then_inc(s_masked, 1)
                dve.wait_ge(s_masked, 2 * n + 2)
                dve.tensor_reduce(s_max[:, t % 2, :], heads(s_sb[:, t % 2, :]), AX_X, ALU.max).then_inc(max_done, 1)

            def p_second(g, t):
                n = TILES * g + t
                if not is0(n):
                    dve.wait_ge(pv_done, n)
                for half in range(2):
                    dve.wait_ge(p_hi_done, 2 * n + half + 1)
                    js = slice(half * 4, half * 4 + 4)
                    dve.tensor_tensor(p_lo[:, js, :].rearrange("p j q -> p (j q)"), ps_p[:, half, :],
                                      p_hi[:, js, :].rearrange("p j q -> p (j q)"), ALU.subtract)\
                        .then_inc(p_lo_done, 1)

            def normalise_o(g, t):
                n = TILES * g + t
                dve.wait_ge(pv_done, n + 1)
                if not is0(n):
                    dve.wait_ge(ot_done, n)
                pv = [ps_c[b * SEQ:(b + 1) * SEQ, :, b * HC * VW:(b + 1) * HC * VW]
                      .rearrange("p c (h d) -> p c h d", d=VW) for b in range(BT)]
                for b in range(BT):
                    dve.reciprocal(sum_inv[b * SEQ:(b + 1) * SEQ], pv[b][:, :, :, D]).then_inc(sum_inverted, 1)
                for b in range(BT):
                    dve.wait_ge(sum_inverted, 2 * n + b + 1)
                    rows_ = slice(b * SEQ, (b + 1) * SEQ)
                    dve.tensor_tensor(o_sb[rows_, :].rearrange("p (c h d) -> p c h d", c=CK, h=HC), pv[b][:, :, :, 0:D],
                                      sum_inv[rows_].unsqueeze(3).broadcast_to([SEQ, CK, HC, D]), ALU.mult)\
                        .then_inc(o_done, 1)

            def o_second(g, t):
                n = TILES * g + t
                dve.wait_ge(o_hi_done, n + 1)
                dve.tensor_tensor(o_lo[:], ps_c[:, 0, 0:C], o_hi[:].bitcast(F32), ALU.subtract)\
                    .then_inc(o_lo_done, 1)

            def x1_add(g, t):
                n = TILES * g + t
                dve.wait_ge(proj_done, n + 1)
                dve.wait_ge(x_biased, n + 1)
                if not is0(g):
                    dve.wait_ge(y_biased, n - TILES + 1)
                dve.tensor_tensor(x1[:, t, :], ps_c[:, 1, 0:C], x_res[:, t, :], ALU.add).then_inc(x1_done, 1)

            def x_clamp(g):
                if not is0(g):
                    dve.wait_ge(x_normed, TILES * g)
                dve.wait_ge(x_powed, g + 1)
                dve.tensor_scalar(x_inv[:], x_pow[:], 1.0 / EPS, None, ALU.min).then_inc(x_inverted, 1)

            def x1_norm(g, t):
                dve.wait_ge(x1_powed, TILES * g + t + 1)
                dve.tensor_scalar(x1_inv[:, t:t + 1], x1_pow[:, t:t + 1], 1.0 / EPS, None, ALU.min)\
                    .then_inc(x1_inverted, 1)
                dve.wait_ge(x1_inverted, TILES * g + t + 1)
                dve.tensor_scalar(x1_nrm[:, t, :], x1[:, t, :], x1_inv[:, t:t + 1], None, ALU.mult)\
                    .then_inc(x1_normed, 1)

            def gated(m, j):
                n = FJ * m + j
                dve.wait_ge(up_done, n + 1)
                dve.wait_ge(silu_done, n + 1)
                dve.scalar_tensor_tensor(out=gate[:, j % 2, :], in0=ps_m[:, 1, :],
                                         scalar=vec[:, MLP_B1 + FJ + j:MLP_B1 + FJ + j + 1], in1=gate[:, j % 2, :],
                                         op0=ALU.add, op1=ALU.mult).then_inc(g_done, 1)

            def g_second(m, j):
                dve.wait_ge(g_hi_done, FJ * m + j + 1)
                dve.tensor_tensor(g_lo[:, j, :], gate[:, j % 2, :], g_hi[:, j, :].bitcast(F32), ALU.subtract)\
                    .then_inc(g_lo_done, 1)

            def y_add(m, t):
                n = TILES * m + t
                dve.wait_ge(down_done, n + 1)
                dve.wait_ge(y_biased, n + 1)
                dve.tensor_tensor(y[:, t, :], ps_m[:, t % 2, 0:C], y[:, t, :], ALU.add).then_inc(ps_m_read, 1)

            def stage_x(g, m, more):
                for t in range(TILES):
                    p_second(g, t)
                    if m is not None:
                        gated(m, 2 * t)
                        g_second(m, 2 * t)
                    if t > 0:
                        x1_norm(g, t - 1)
                    if more and t == 3:
                        x_clamp(g + 1)
                    normalise_o(g, t)
                    if m is not None:
                        gated(m, 2 * t + 1)
                    o_second(g, t)
                    if m is not None:
                        g_second(m, 2 * t + 1)
                    if t + 2 < TILES:
                        v_rests(g, t + 2)
                        mask_and_max(g, t + 2)
                    x1_add(g, t)
                    if m is None:
                        for s in range(2 + 2 * t, min(4 + 2 * t, W_CHUNKS)):
                            w_split_lo(s)

            def stage_y(g, m, more):
                if more:
                    adaln1(g + 1)
                x1_norm(g, TILES - 1)
                if m is not None:
                    y_add(m, 0)
                    y_add(m, 1)
                adaln2(g, more)
                if m is not None:
                    y_add(m, 2)
                if more:
                    v_rests(g + 1, 0)
                    mask_and_max(g + 1, 0)
                if m is not None:
                    y_add(m, 3)
                if more:
                    v_rests(g + 1, 1)
                    mask_and_max(g + 1, 1)

            x_clamp(0)
            modulation()
            w_split_lo(0)
            adaln1(0)
            w_split_lo(1)
            dve.wait_ge(mask_step, 6)
            for t in range(2):
                v_rests(0, t)
                mask_and_max(0, t)
            stage_x(0, None, True)
            stage_y(0, None, True)
            with dve.Fori(1, GROUPS - 1) as g:
                stage_x(g, g - 1, True)
                stage_y(g, g - 1, True)
            last = GROUPS - 1
            stage_x(last, last - 1, False)
            stage_y(last, last - 1, False)
            for j in range(FJ):
                gated(last, j)
                g_second(last, j)
            for t in range(TILES):
                y_add(last, t)


def kernel(x, cond_1024, mask_BxS_ik0, L0_cond_norm_w, L0_cond_scale_w, L0_cond_scale_b, L0_cond_shift_w,
           L0_cond_shift_b, L0_cond_qkv_w, L0_cond_proj_w, L0_cond_proj_b, L0_cond_mlp_w1, L0_cond_mlp_b1,
           L0_cond_mlp_w2, L0_cond_mlp_b2):
    import numpy as np
    import concourse.bacc as bacc
    from concourse.bass_utils import run_bass_kernel_spmd

    def by_input(w):
        w = np.asarray(w)
        return w.T.reshape(-1, P, w.shape[0]).transpose(1, 0, 2).reshape(P, -1)

    def columns(v):
        return np.asarray(v).reshape(-1, P).T

    qkv = np.asarray(L0_cond_qkv_w)
    arrays = {
        "x": np.asarray(x).reshape(BATCH * SEQ, C),
        "cond_t": np.asarray(cond_1024).T.reshape(CK, P, BATCH).transpose(1, 0, 2),
        "mask": np.asarray(mask_BxS_ik0),
        "weights": np.concatenate([by_input(qkv[:2 * C]), by_input(qkv[2 * C:]), by_input(L0_cond_proj_w),
                                   by_input(L0_cond_mlp_w1), by_input(L0_cond_mlp_w2)], axis=1),
        "mod_w": np.stack([by_input(L0_cond_scale_w), by_input(L0_cond_shift_w)], axis=1).reshape(P, 2, CK, C),
        "vecs": np.concatenate([columns(v) for v in (L0_cond_scale_b, L0_cond_shift_b, L0_cond_norm_w,
                                                     L0_cond_mlp_b1)], axis=1),
        "rows": np.stack([np.asarray(L0_cond_proj_b), np.asarray(L0_cond_mlp_b2)]),
    }
    nc = bacc.Bacc("TRN2", target_bir_lowering=False, num_devices=1)
    args = {}
    for name, a in arrays.items():
        arrays[name] = np.ascontiguousarray(a)
        args[name] = nc.dram_tensor(name, a.shape, mybir.dt.from_np(a.dtype), kind="ExternalInput").ap()
    args["out"] = nc.dram_tensor("out", (BATCH * SEQ, C), F32, kind="ExternalOutput").ap()
    block_kernel(nc, **args)
    r = run_bass_kernel_spmd(nc, [arrays], core_ids=[0])
    return r.results[0]["out"].reshape(BATCH, SEQ, C)
```

```python
from contextlib import ExitStack

import concourse.bass as bass
from concourse import mybir

F32 = mybir.dt.float32
F32R = mybir.dt.float32r
BF16 = mybir.dt.bfloat16
F16 = mybir.dt.float16
I32 = mybir.dt.int32
ALU = mybir.AluOpType
ACT = mybir.ActivationFunctionType
AX_X = mybir.AxisListType.X

P = 128
BATCH, SEQ, C = 32, 64, 256
HEADS = 16
D = C // HEADS
F = 4 * C
TILES = 4
GTOK = TILES * P
GROUPS = BATCH * SEQ // GTOK
BT = P // SEQ
BG = TILES * BT
NT = GROUPS * TILES
CK = C // P
HC = HEADS // CK
FJ = F // P
PAIRS = HEADS // 2
SCALE = float(D) ** -0.5
EPS = 1e-6
MASKED = -1.0e30
EXP_SHIFT = 9.7
VW = D + 1

WCH = 1024
QK_AT, V_AT = 0, CK * 2 * C
PR_AT = V_AT + CK * C
W1_AT = PR_AT + CK * C
W2_AT = W1_AT + CK * 2 * F
W_COLS = W2_AT + FJ * C
W_CHUNKS = W_COLS // WCH
SCALE_B, SHIFT_B, NORM_W, MLP_B1 = 0, CK, 2 * CK, 3 * CK
VEC_COLS = 3 * CK + 2 * FJ


def block_kernel(nc, x, cond_t, mask, weights, mod_w, vecs, rows, out):
    x_v = x.rearrange("(g t p) c -> g p t c", g=GROUPS, t=TILES)
    out_v = out.rearrange("(n p) c -> n p c", p=P)

    with ExitStack() as ctx:
        def sb(name, shape, dt=F32):
            return ctx.enter_context(nc.sbuf_tensor(name, shape, dt))

        def ps(name, shape):
            return ctx.enter_context(nc.psum_tensor(name, shape, F32))

        def sem(name):
            return ctx.enter_context(nc.semaphore(name))

        w_hi = sb("w_hi", [P, W_COLS], F32R)
        w_lo = sb("w_lo", [P, W_COLS], F32R)
        w_raw = sb("w_raw", [P, 2, WCH])
        vec = sb("vec", [P, VEC_COLS])
        proj_b = sb("proj_b", [P, C])
        mlp_b2 = sb("mlp_b2", [P, C])
        ident = sb("ident", [P, P])
        head_rows = sb("head_rows", [P, HC])
        exp_shift = sb("exp_shift", [P, 1])
        neg_half = sb("neg_half", [P, TILES])
        cond = sb("cond", [P, CK, BATCH])
        scale_w = sb("scale_w", [P, CK, BATCH])
        shift = sb("shift", [P, CK, BATCH])
        mask_add = sb("mask_add", [P, NT, SEQ])
        all_masked = sb("all_masked", [P, NT])
        score_mul = sb("score_mul", [P, NT])
        x_in = sb("x_in", [P, TILES, C])
        x_nrm = sb("x_nrm", [P, TILES, C])
        x_res = sb("x_res", [P, TILES, C])
        x_ssq = sb("x_ssq", [P, TILES])
        x_pow = sb("x_pow", [P, TILES])
        x_inv = sb("x_inv", [P, TILES])
        x1 = sb("x1", [P, TILES, C])
        x1_nrm = sb("x1_nrm", [P, TILES, C])
        x1_ssq = sb("x1_ssq", [P, TILES])
        x1_pow = sb("x1_pow", [P, TILES])
        x1_inv = sb("x1_inv", [P, TILES])
        y = sb("y", [P, TILES, C])
        h_full = sb("h_full", [P, CK, GTOK])
        h1_hi = sb("h1_hi", [P, CK, GTOK], F32R)
        h1_lo = sb("h1_lo", [P, CK, GTOK], F32R)
        h2_hi = sb("h2_hi", [P, CK, GTOK], F32R)
        h2_lo = sb("h2_lo", [P, CK, GTOK], F32R)
        q_t = sb("q_t", [P, CK, GTOK])
        k_t = sb("k_t", [P, CK, GTOK])
        k_diag = sb("k_diag", [P, 2, CK, BT, HC * SEQ])
        s_sb = sb("s_sb", [P, 2, HEADS * SEQ])
        s_max = sb("s_max", [P, 2, HEADS])
        p_hi = sb("p_hi", [P, PAIRS, P], F16)
        p_lo = sb("p_lo", [P, PAIRS, P], F16)
        v_part = sb("v_part", [P, 3, PAIRS, 2, D], BF16)
        v_rest = sb("v_rest", [P, C])
        v_diag = sb("v_diag", [P, 2, PAIRS, 3, BT, 2, VW], BF16)
        sum_inv = sb("sum_inv", [P, 2, HC])
        o_sb = sb("o_sb", [P, C])
        o_hi = sb("o_hi", [P, C], F32R)
        o_lo = sb("o_lo", [P, C], F32R)
        gate = sb("gate", [P, 2, GTOK])
        half_b1 = sb("half_b1", [P, FJ])
        g_hi = sb("g_hi", [P, FJ, GTOK], F32R)
        g_lo = sb("g_lo", [P, FJ, GTOK], F32R)
        gate_tanh = w_raw[:, :, 0:GTOK]
        cond_tanh = y[:, 0, 0:CK * BATCH].rearrange("p (k b) -> p k b", k=CK)
        table_warm = y[:, 1, 0:1]
        mask_raw = s_sb[:, 0, :].bitcast(I32).rearrange("p (n k) -> p n k", k=SEQ)
        mod_sb = s_sb[:, 1, :].rearrange("p (s k n) -> p s k n", s=2, k=CK)

        ps_s = ps("ps_s", [P, 2, 512])
        ps_p = ps("ps_p", [P, 2, 512])
        ps_c = ps("ps_c", [P, 2, 512])
        ps_m = ps("ps_m", [P, 2, 512])

        wqk = [w[:, QK_AT:V_AT].rearrange("p (k n) -> p k n", k=CK) for w in (w_hi, w_lo)]
        wv = [w[:, V_AT:PR_AT].rearrange("p (k n) -> p k n", k=CK) for w in (w_hi, w_lo)]
        wpr = [w[:, PR_AT:W1_AT].rearrange("p (k n) -> p k n", k=CK) for w in (w_hi, w_lo)]
        w1 = [w[:, W1_AT:W2_AT].rearrange("p (k n) -> p k n", k=CK) for w in (w_hi, w_lo)]
        w2 = [w[:, W2_AT:W_COLS].rearrange("p (j n) -> p j n", j=FJ) for w in (w_hi, w_lo)]
        h1, h2, o_t, g_t = (h1_hi, h1_lo), (h2_hi, h2_lo), (o_hi, o_lo), (g_hi, g_lo)
        PARTS = ((0, 0), (0, 1), (1, 0))

        vec_loaded, rows_loaded, cond_loaded = sem("vec_loaded"), sem("rows_loaded"), sem("cond_loaded")
        mask_loaded, mod_loaded = sem("mask_loaded"), sem("mod_loaded")
        w_loaded = [sem("w_loaded_even"), sem("w_loaded_odd")]
        w_hi_done, w_lo_done = sem("w_hi_done"), sem("w_lo_done")
        ident_ready, consts_ready = sem("ident_ready"), sem("consts_ready")
        vdiag_ready, mask_step, mod_step = sem("vdiag_ready"), sem("mask_step"), sem("mod_step")
        cond_silu, mod_done, heads_ready = sem("cond_silu"), sem("mod_done"), sem("heads_ready")
        half_b1_ready, cond_tanh_done = sem("half_b1_ready"), sem("cond_tanh_done")
        w_hi_mlp_done, w_lo_mlp_done = sem("w_hi_mlp_done"), sem("w_lo_mlp_done")
        x_loaded, x_squared, x_powed = sem("x_loaded"), sem("x_squared"), sem("x_powed")
        x_inverted, x_normed, x_biased = sem("x_inverted"), sem("x_normed"), sem("x_biased")
        xt_done, h1_scaled, h1_full = sem("xt_done"), sem("h1_scaled"), sem("h1_full")
        h1_hi_done, h1_lo_done = sem("h1_hi_done"), sem("h1_lo_done")
        k_done, k_copied, q_done, q_copied = sem("k_done"), sem("k_copied"), sem("q_done"), sem("q_copied")
        kdiag_built, s_done, s_masked = sem("kdiag_built"), sem("s_done"), sem("s_masked")
        max_done, max_subtracted, exp_done = sem("max_done"), sem("max_subtracted"), sem("exp_done")
        pt_done, p_hi_done, p_lo_done = sem("pt_done"), sem("p_hi_done"), sem("p_lo_done")
        v_done, v1_done, v_rest_done = sem("v_done"), sem("v1_done"), sem("v_rest_done")
        v2_done, v3_done, vdiag_built = sem("v2_done"), sem("v3_done"), sem("vdiag_built")
        pv_done, sum_inverted, o_done = sem("pv_done"), sem("sum_inverted"), sem("o_done")
        ot_done, o_hi_done, o_lo_done = sem("ot_done"), sem("o_hi_done"), sem("o_lo_done")
        proj_done, x1_done = sem("proj_done"), sem("x1_done")
        x1_squared, x1_powed, x1_inverted = sem("x1_squared"), sem("x1_powed"), sem("x1_inverted")
        x1_normed, y_biased = sem("x1_normed"), sem("y_biased")
        x1t_done, h2_scaled, h2_full = sem("x1t_done"), sem("h2_scaled"), sem("h2_full")
        h2_hi_done, h2_lo_done = sem("h2_hi_done"), sem("h2_lo_done")
        gate_done, up_done, gate_read = sem("gate_done"), sem("up_done"), sem("gate_read")
        up_read, g_done, g_hi_done = sem("up_read"), sem("g_done"), sem("g_hi_done")
        g_lo_even, g_lo_odd = sem("g_lo_even"), sem("g_lo_odd")
        down_done = sem("down_done")
        ps_m_read = sem("ps_m_read")
        y_free = sem("y_free")

        block = ctx.enter_context(nc.Block())
        is0 = lambda g: isinstance(g, int) and g == 0

        @block.sync
        def _(sp):
            def load_x(g):
                if not is0(g):
                    sp.wait_ge(x_normed, TILES * g)
                    sp.wait_ge(x_biased, TILES * g)
                src = x_v[g] if isinstance(g, int) else x_v[bass.ds(g, 1)].rearrange("a p t c -> (a p) t c")
                sp.dma_start(x_in[:], src).then_inc(x_loaded, 16)

            def load_w(s):
                if 2 <= s < 4:
                    sp.wait_ge(w_lo_done, s - 1)
                elif s >= 4:
                    sp.wait_ge(w_lo_mlp_done, s - 3)
                sp.dma_start(w_raw[:, s % 2, :], weights[:, s * WCH:(s + 1) * WCH]).then_inc(w_loaded[s % 2], 16)

            load_x(0)
            load_w(0)
            load_w(1)
            sp.dma_start(proj_b[:], rows[0:1, :].broadcast_to([P, C])).then_inc(rows_loaded, 16)
            sp.dma_start(mlp_b2[:], rows[1:2, :].broadcast_to([P, C])).then_inc(y_free, 16)
            for s in range(2, W_CHUNKS):
                load_w(s)
            load_x(1)

            def store_y(g):
                for t in range(TILES):
                    n = TILES * g + t
                    sp.wait_ge(ps_m_read, n + 2)
                    dst = out_v[n] if isinstance(n, int) else out_v[bass.ds(n, 1)].rearrange("a p c -> (a p) c")
                    sp.dma_start(dst, y[:, t, :]).then_inc(y_free, 16)

            with sp.Fori(1, GROUPS - 1) as g:
                load_x(g + 1)
                store_y(g - 1)
            store_y(GROUPS - 2)
            store_y(GROUPS - 1)
            sp.wait_ge(y_free, 16 * NT + 16)

        @block.tensor
        def _(pe):
            def product(dst, lhs, rhs, lhs_at, rhs_at, n):
                for k in range(n):
                    for a, b in PARTS:
                        last = pe.matmul(dst, lhs[a][:, k, lhs_at], rhs[b][:, k, rhs_at],
                                         start=(k == 0 and (a, b) == PARTS[0]),
                                         stop=(k == n - 1 and (a, b) == PARTS[-1]))
                return last

            def modulation():
                pe.wait_ge(cond_silu, 1)
                pe.wait_ge(mod_loaded, 16)
                for s in range(2):
                    for m in range(CK):
                        for k in range(CK):
                            last = pe.matmul(ps_m[:, s, m * BATCH:(m + 1) * BATCH],
                                             mod_sb[:, s, k, m * P:(m + 1) * P], cond[:, k, :],
                                             start=(k == 0), stop=(k == CK - 1))
                    last.then_inc(mod_done, 1)

            def x_transposed(g):
                pe.wait_ge(x_normed, TILES * g + TILES)
                for c in range(CK):
                    if not is0(g):
                        pe.wait_ge(p_lo_done, 2 * TILES * g)
                    for t in range(TILES):
                        last = pe.transpose(ps_p[:, c, t * P:(t + 1) * P], x_nrm[:, t, c * P:(c + 1) * P], ident[:])
                    last.then_inc(xt_done, 1)

            def k_proj(g):
                pe.wait_ge(h1_lo_done, CK * g + CK)
                for c in range(CK):
                    if not is0(g):
                        pe.wait_ge(s_masked, 2 * TILES * g - 1 + c)
                    product(ps_s[:, c, :], wqk, h1, slice(C + c * P, C + (c + 1) * P), slice(0, GTOK), CK)\
                        .then_inc(k_done, 1)

            def q_proj(g):
                for c in range(CK):
                    pe.wait_ge(k_copied, CK * g + c + 1)
                    product(ps_s[:, c, :], wqk, h1, slice(c * P, (c + 1) * P), slice(0, GTOK), CK)\
                        .then_inc(q_done, 1)

            def v_proj(g, t, behind=2):
                n = TILES * g + t
                if t == 0:
                    pe.wait_ge(h1_scaled, CK * g + CK)
                elif t == 1:
                    pe.wait_ge(v_rest_done, n)
                else:
                    pe.wait_ge(p_lo_done, 2 * (n - behind) + 1)
                product(ps_p[:, 0, 0:C], h1, wv, slice(t * P, (t + 1) * P), slice(0, C), CK).then_inc(v_done, 1)

            def scores(g, t):
                n = TILES * g + t
                pe.wait_ge(q_copied, CK * g + CK)
                for c in range(CK):
                    pe.wait_ge(kdiag_built, 2 * n + c + 1)
                    if t > 0:
                        pe.wait_ge(s_masked, 2 * n - 1 + c)
                    for b in range(BT):
                        last = pe.matmul(ps_s[b * SEQ:(b + 1) * SEQ, c, :],
                                         q_t[:, c, t * P + b * SEQ:t * P + (b + 1) * SEQ],
                                         k_diag[:, t % 2, c, b, :], start=True, stop=True)
                    last.then_inc(s_done, 1)

            def p_transposed(g, t, v_tiles):
                n = TILES * g + t
                pe.wait_ge(exp_done, n + 1)
                pe.wait_ge(v_rest_done, TILES * g + v_tiles)
                if t > 0:
                    pe.wait_ge(p_lo_done, 2 * n)
                for half in range(2):
                    for j in range(4):
                        at = (half * 4 + j) * P
                        last = pe.transpose(ps_p[:, half, j * P:(j + 1) * P], s_sb[:, t % 2, at:at + P], ident[:])
                    last.then_inc(pt_done, 1)

            def p_times_v(g, t):
                n = TILES * g + t
                pe.wait_ge(vdiag_built, 4 * n + 4)
                if t > 0:
                    pe.wait_ge(o_lo_done, n)
                    pe.wait_ge(x1_done, n)
                elif not is0(g):
                    pe.wait_ge(h2_scaled, CK * g)
                for half in range(2):
                    pe.wait_ge(p_lo_done, 2 * n + half + 1)
                    for j in range(4):
                        pair = half * 4 + j
                        dst = ps_c[:, half, 0:BT * 4 * 2 * VW]\
                            .rearrange("p (b j n) -> p b j n", b=BT, j=4)[:, :, j, :]
                        terms = [(p_hi, 0), (p_hi, 1), (p_hi, 2), (p_lo, 0), (p_lo, 1)]
                        for i, (part, v) in enumerate(terms):
                            last = pe.matmul(dst, part[:, pair, :],
                                             v_diag[:, t % 2, pair, v].rearrange("p b h n -> p b (h n)"),
                                             start=(i == 0), stop=(i == len(terms) - 1))
                last.then_inc(pv_done, 1)

            def o_transposed(g, t):
                pe.wait_ge(o_done, 2 * (TILES * g + t) + 2)
                for c in range(CK):
                    last = pe.transpose(ps_c[:, 0, c * P:(c + 1) * P], o_sb[:, c * P:(c + 1) * P], ident[:])
                last.then_inc(ot_done, 1)

            def projection(g, t):
                pe.wait_ge(o_lo_done, TILES * g + t + 1)
                o_v = [o[:, :].rearrange("p (k n) -> p k n", k=CK) for o in o_t]
                product(ps_c[:, 1, 0:C], o_v, wpr, slice(0, P), slice(0, C), CK).then_inc(proj_done, 1)

            def x1_transposed(g):
                pe.wait_ge(x1_normed, TILES * g + TILES)
                pe.wait_ge(o_lo_done, TILES * g + TILES)
                pe.wait_ge(x1_done, TILES * g + TILES)
                for c in range(CK):
                    for t in range(TILES):
                        last = pe.transpose(ps_c[:, c, t * P:(t + 1) * P], x1_nrm[:, t, c * P:(c + 1) * P], ident[:])
                    last.then_inc(x1t_done, 1)

            def mlp_gate(m, j, bank=ps_m, ahead=0):
                n = FJ * m + j
                if j == 0:
                    pe.wait_ge(h2_lo_done, CK * m + CK)
                    pe.wait_ge(ps_m_read, TILES * m + 1)
                elif j > ahead:
                    pe.wait_ge(gate_read, n - ahead)
                product(bank[:, 0, :], w1, h2, slice(j * P, (j + 1) * P), slice(0, GTOK), CK).then_inc(gate_done, 1)

            def mlp_up(m, j, bank=ps_m, ahead=0):
                n = FJ * m + j
                if j > ahead:
                    pe.wait_ge(up_read, n - ahead)
                product(bank[:, 1, :], w1, h2, slice(F + j * P, F + (j + 1) * P), slice(0, GTOK), CK)\
                    .then_inc(up_done, 1)

            def mlp_down(m, t):
                n = TILES * m + t
                if t == 0:
                    pe.wait_ge(gate_read, FJ * m + FJ)
                elif t == 1:
                    pe.wait_ge(up_read, FJ * m + FJ)
                else:
                    pe.wait_ge(ps_m_read, n)
                for j in range(FJ):
                    if t == 0:
                        pe.wait_ge((g_lo_even, g_lo_odd)[j % 2], FJ // 2 * m + j // 2 + 1)
                    for a, b in PARTS:
                        last = pe.matmul(ps_m[:, t % 2, 0:C], g_t[a][:, j, t * P:(t + 1) * P], w2[b][:, j, :],
                                         start=(j == 0 and (a, b) == PARTS[0]),
                                         stop=(j == FJ - 1 and (a, b) == PARTS[-1]))
                last.then_inc(down_done, 1)

            def stage_x(g, m):
                for t in range(TILES):
                    mlp_gate(m, 2 * t)
                    p_transposed(g, t, min(t + 2, TILES))
                    mlp_up(m, 2 * t)
                    mlp_gate(m, 2 * t + 1)
                    p_times_v(g, t)
                    mlp_up(m, 2 * t + 1)
                    o_transposed(g, t)
                    if t + 2 < TILES:
                        v_proj(g, t + 2)
                        scores(g, t + 2)
                    projection(g, t)

            def stage_x_alone(g):
                p_transposed(g, 0, 2)
                for t in range(TILES):
                    if t + 2 < TILES:
                        scores(g, t + 2)
                    p_times_v(g, t)
                    if t + 1 < TILES:
                        p_transposed(g, t + 1, max(t + 1, 1) + 1)
                    o_transposed(g, t)
                    projection(g, t)
                    if t + 2 < TILES:
                        v_proj(g, t + 2, behind=1)

            def stage_y(g, m, more):
                if more:
                    x_transposed(g + 1)
                if m is not None:
                    mlp_down(m, 0)
                    mlp_down(m, 1)
                if more:
                    k_proj(g + 1)
                x1_transposed(g)
                if more:
                    q_proj(g + 1)
                if m is not None:
                    mlp_down(m, 2)
                if more:
                    v_proj(g + 1, 0)
                    scores(g + 1, 0)
                if m is not None:
                    mlp_down(m, 3)
                if more:
                    v_proj(g + 1, 1)
                    scores(g + 1, 1)

            pe.wait_ge(ident_ready, 2)
            modulation()
            x_transposed(0)
            pe.wait_ge(w_lo_done, 1)
            k_proj(0)
            q_proj(0)
            pe.wait_ge(w_lo_done, 2)
            for t in range(2):
                v_proj(0, t)
                scores(0, t)
            pe.wait_ge(vdiag_ready, 1)
            stage_x_alone(0)
            stage_y(0, None, True)
            pe.wait_ge(w_lo_mlp_done, W_CHUNKS - 2)
            with pe.Fori(1, GROUPS - 1) as g:
                stage_x(g, g - 1)
                stage_y(g, g - 1, True)
            last = GROUPS - 1
            stage_x(last, last - 1)
            stage_y(last, last - 1, False)
            for j in range(FJ):
                mlp_gate(last, j, (ps_m, ps_s)[j % 2], 1)
                mlp_up(last, j, (ps_m, ps_s)[j % 2], 1)
            for t in range(TILES):
                mlp_down(last, t)

        @block.scalar
        def _(act):
            act.dma_start(cond[:], cond_t).then_inc(cond_loaded, 16)
            act.dma_start(mod_sb, mod_w).then_inc(mod_loaded, 16)
            act.dma_start(vec[:], vecs).then_inc(vec_loaded, 16)
            for b in range(BT):
                src = mask.rearrange("(n b) k -> b n k", b=BT)[b:b + 1].broadcast_to([SEQ, NT, SEQ])
                act.dma_start(mask_raw[b * SEQ:(b + 1) * SEQ], src).then_inc(mask_loaded, 16)
            act.wait_ge(consts_ready, 2)
            act.activation(table_warm[:], exp_shift[:], ACT.Exp)
            act.wait_ge(cond_loaded, 16)
            act.activation(cond_tanh[:], cond[:], ACT.Tanh, scale=0.5).then_inc(cond_tanh_done, 1)

            def w_split_hi(s):
                act.wait_ge(w_loaded[s % 2], 16 * (s // 2 + 1))
                act.activation(w_hi[:, s * WCH:(s + 1) * WCH], w_raw[:, s % 2, :], ACT.Copy)\
                    .then_inc(w_hi_mlp_done, 1)

            def x_squares(g):
                act.wait_ge(x_loaded, 16 * g + 16)
                if not is0(g):
                    act.wait_ge(xt_done, CK * g)
                    act.wait_ge(x_inverted, g)
                for t in range(TILES):
                    act.activation(x_nrm[:, t, :], x_in[:, t, :], ACT.Square, scale=1.0 / 16.0,
                                   accum_out=x_ssq[:, t:t + 1]).then_inc(x_squared, 1)

            def x_norms(g):
                act.wait_ge(x_inverted, g + 1)
                act.wait_ge(x_squared, TILES * g + TILES)
                for t in range(TILES):
                    act.activation(x_nrm[:, t, :], x_in[:, t, :], ACT.Copy, scale=x_inv[:, t:t + 1])\
                        .then_inc(x_normed, 1)

            def h1_parts(g):
                if not is0(g):
                    act.wait_ge(v_done, TILES * g)
                for c in range(CK):
                    act.wait_ge(h1_full, CK * g + c + 1)
                    act.activation(h1_hi[:, c, :], h_full[:, c, :], ACT.Copy).then_inc(h1_hi_done, 1)

            def h2_parts(g):
                if not is0(g):
                    act.wait_ge(up_done, FJ * g)
                for c in range(CK):
                    act.wait_ge(h2_full, CK * g + c + 1)
                    act.activation(h2_hi[:, c, :], h_full[:, c, :], ACT.Copy).then_inc(h2_hi_done, 1)

            def k_copy(g):
                if not is0(g):
                    act.wait_ge(kdiag_built, 2 * TILES * g)
                for c in range(CK):
                    act.wait_ge(k_done, CK * g + c + 1)
                    act.activation(k_t[:, c, :], ps_s[:, c, :], ACT.Copy).then_inc(k_copied, 1)

            def q_copy(g):
                if not is0(g):
                    act.wait_ge(s_done, 2 * TILES * g)
                for c in range(CK):
                    act.wait_ge(q_done, CK * g + c + 1)
                    act.activation(q_t[:, c, :], ps_s[:, c, :], ACT.Copy).then_inc(q_copied, 1)

            def v_first(g, t):
                n = TILES * g + t
                act.wait_ge(v_done, n + 1)
                if not is0(n):
                    act.wait_ge(vdiag_built, 4 * n)
                act.activation(v_part[:, 0].rearrange("p j h d -> p (j h d)"), ps_p[:, 0, 0:C], ACT.Copy)\
                    .then_inc(v1_done, 1)

            def v_placed(g, t):
                n = TILES * g + t
                act.wait_ge(v3_done, n + 1)
                if isinstance(n, int) and n < 2:
                    act.wait_ge(vdiag_ready, 1)
                else:
                    act.wait_ge(pv_done, n - 1)
                for b in range(BT):
                    for hp in range(2):
                        act.activation(v_diag[hp * SEQ:(hp + 1) * SEQ, t % 2, :, :, b, hp, 0:D],
                                       v_part[b * SEQ:(b + 1) * SEQ, :, :, hp, :].rearrange("p i j d -> p j i d"),
                                       ACT.Copy).then_inc(vdiag_built, 1)

            def exps(g, t):
                n = TILES * g + t
                act.wait_ge(max_subtracted, n + 1)
                act.activation(s_sb[:, t % 2, :], s_sb[:, t % 2, :], ACT.Exp, bias=exp_shift[:, 0:1])\
                    .then_inc(exp_done, 1)

            def p_first(g, t):
                n = TILES * g + t
                if not is0(n):
                    act.wait_ge(pv_done, n)
                for half in range(2):
                    act.wait_ge(pt_done, 2 * n + half + 1)
                    act.activation(p_hi[:, half * 4:half * 4 + 4, :].rearrange("p j q -> p (j q)"),
                                   ps_p[:, half, :], ACT.Copy).then_inc(p_hi_done, 1)

            def o_first(g, t):
                n = TILES * g + t
                act.wait_ge(ot_done, n + 1)
                if not is0(n):
                    act.wait_ge(proj_done, n)
                act.activation(o_hi[:], ps_c[:, 0, 0:C], ACT.Copy).then_inc(o_hi_done, 1)

            def x1_squares(g, t):
                n = TILES * g + t
                act.wait_ge(x1_done, n + 1)
                if not is0(g):
                    act.wait_ge(x1t_done, CK * g)
                act.activation(x1_nrm[:, t, :], x1[:, t, :], ACT.Square, scale=1.0 / 16.0,
                               accum_out=x1_ssq[:, t:t + 1]).then_inc(x1_squared, 1)

            def x1_norm(g, t):
                act.wait_ge(x1_inverted, TILES * g + t + 1)
                act.wait_ge(x1_squared, TILES * g + t + 1)
                act.activation(x1_nrm[:, t, :], x1[:, t, :], ACT.Copy, scale=x1_inv[:, t:t + 1])\
                    .then_inc(x1_normed, 1)

            def gate_parts(m, j, bank=ps_m):
                n = FJ * m + j
                act.wait_ge(gate_done, n + 1)
                if j >= 2:
                    act.wait_ge((g_lo_even, g_lo_odd)[j % 2], FJ // 2 * m + j // 2)
                act.activation(gate_tanh[:, j % 2, :], bank[:, 0, :], ACT.Tanh, bias=half_b1[:, j:j + 1], scale=0.5)
                act.activation(gate[:, j % 2, :], bank[:, 0, :], ACT.Identity, bias=half_b1[:, j:j + 1], scale=0.5)\
                    .then_inc(gate_read, 1)

            def g_first(m, j):
                n = FJ * m + j
                act.wait_ge(g_done, n + 1)
                act.activation(g_hi[:, j, :], gate[:, j % 2, :], ACT.Copy).then_inc(g_hi_done, 1)

            def stage_x(g, m, more):
                for t in range(TILES):
                    gate_parts(m, 2 * t)
                    p_first(g, t)
                    if t > 0:
                        x1_squares(g, t - 1)
                    if t + 1 < TILES:
                        v_placed(g, t + 1)
                    gate_parts(m, 2 * t + 1)
                    g_first(m, 2 * t)
                    if t > 0:
                        x1_norm(g, t - 1)
                    if more and t == 3:
                        x_norms(g + 1)
                    o_first(g, t)
                    if t + 1 < TILES:
                        exps(g, t + 1)
                    g_first(m, 2 * t + 1)
                    if t + 2 < TILES:
                        v_first(g, t + 2)
                    if more and t == 2:
                        x_squares(g + 1)

            def stage_x_alone(g):
                for t in range(TILES):
                    p_first(g, t)
                    if t + 1 < TILES:
                        if t > 0:
                            v_first(g, t + 1)
                        v_placed(g, t + 1)
                    if t > 0:
                        x1_squares(g, t - 1)
                    if t + 1 < TILES:
                        exps(g, t + 1)
                    if t > 0:
                        x1_norm(g, t - 1)
                    o_first(g, t)
                    if t == 2:
                        x_squares(g + 1)
                    if t == 3:
                        x_norms(g + 1)
                    for s in range(2 + 2 * t, min(4 + 2 * t, W_CHUNKS)):
                        w_split_hi(s)

            def stage_y(g, more):
                if more:
                    h1_parts(g + 1)
                x1_squares(g, TILES - 1)
                x1_norm(g, TILES - 1)
                if more:
                    k_copy(g + 1)
                h2_parts(g)
                if more:
                    q_copy(g + 1)
                    v_first(g + 1, 0)
                    v_placed(g + 1, 0)
                    exps(g + 1, 0)
                    v_first(g + 1, 1)

            x_squares(0)
            x_norms(0)
            h1_parts(0)
            k_copy(0)
            q_copy(0)
            v_first(0, 0)
            v_placed(0, 0)
            exps(0, 0)
            v_first(0, 1)
            stage_x_alone(0)
            stage_y(0, True)
            act.wait_ge(half_b1_ready, 1)
            with act.Fori(1, GROUPS - 1) as g:
                stage_x(g, g - 1, True)
                stage_y(g, True)
            last = GROUPS - 1
            stage_x(last, last - 1, False)
            stage_y(last, False)
            for j in range(FJ):
                gate_parts(last, j, (ps_m, ps_s)[j % 2])
                if j > 0:
                    g_first(last, j - 1)
            g_first(last, FJ - 1)

        @block.gpsimd
        def _(pool):
            pool.memset(ident[:], 0.0).then_inc(ident_ready, 1)
            pool.memset(neg_half[:], -0.5).then_inc(consts_ready, 1)
            pool.memset(exp_shift[:], EXP_SHIFT).then_inc(consts_ready, 1)
            pool.wait_ge(ident_ready, 1)
            pool.affine_select(out=ident[:], in_=ident[:], compare_op=ALU.not_equal, fill=1.0, base=0,
                               pattern=[[-1, P]], channel_multiplier=1).then_inc(ident_ready, 1)

            def x_power(g):
                if not is0(g):
                    pool.wait_ge(x_inverted, g)
                pool.wait_ge(x_squared, TILES * g + TILES)
                pool.tensor_tensor(x_pow[:], x_ssq[:], neg_half[:], ALU.pow).then_inc(x_powed, 1)

            def x_bias(g):
                pool.wait_ge(x_loaded, 16 * g + 16)
                if not is0(g):
                    pool.wait_ge(x1_done, TILES * g)
                for t in range(TILES):
                    pool.tensor_tensor(x_res[:, t, :], x_in[:, t, :], proj_b[:], ALU.add).then_inc(x_biased, 1)

            def k_diagonal(g, t):
                n = TILES * g + t
                if isinstance(n, int) and n < 2:
                    pass
                else:
                    pool.wait_ge(s_done, 2 * n - 2)
                for c in range(CK):
                    dst = k_diag[:, t % 2, c].rearrange("p b (h k) -> p b h k", h=HC)
                    src = k_t[:, c, t * P:(t + 1) * P].rearrange("p (b k) -> p b k", b=BT)\
                        .unsqueeze(2).broadcast_to([P, BT, HC, SEQ])
                    of_head = head_rows[:].unsqueeze(1).unsqueeze(3).broadcast_to([P, BT, HC, SEQ])
                    pool.wait_ge(k_copied, CK * g + c + 1)
                    pool.tensor_tensor(dst, src, of_head, ALU.mult).then_inc(kdiag_built, 1)

            def subtract_max(g, t):
                n = TILES * g + t
                pool.wait_ge(max_done, n + 1)
                s_v = s_sb[:, t % 2, :].rearrange("p (h k) -> p h k", h=HEADS)
                pool.tensor_tensor(s_v, s_v, s_max[:, t % 2, :].unsqueeze(2).broadcast_to([P, HEADS, SEQ]),
                                   ALU.subtract).then_inc(max_subtracted, 1)

            def x1_power(g, t):
                n = TILES * g + t
                pool.wait_ge(x1_squared, n + 1)
                if not is0(g):
                    pool.wait_ge(x1_inverted, n - TILES + 1)
                pool.tensor_tensor(x1_pow[:, t:t + 1], x1_ssq[:, t:t + 1], neg_half[:, t:t + 1], ALU.pow)\
                    .then_inc(x1_powed, 1)

            def y_bias(g, t):
                n = TILES * g + t
                pool.wait_ge(x1_done, n + 1)
                pool.wait_ge(y_free, 16 * TILES * g + 16)
                pool.tensor_tensor(y[:, t, :], x1[:, t, :], mlp_b2[:], ALU.add).then_inc(y_biased, 1)

            def g_second(m, j):
                pool.wait_ge(g_hi_done, FJ * m + j + 1)
                pool.tensor_tensor(g_lo[:, j, :], gate[:, j % 2, :], g_hi[:, j, :].bitcast(F32), ALU.subtract)\
                    .then_inc(g_lo_odd, 1)

            def w_split_lo(s):
                pool.wait_ge(w_hi_mlp_done, s - 1)
                cols = slice(s * WCH, (s + 1) * WCH)
                pool.tensor_tensor(w_lo[:, cols], w_raw[:, s % 2, :], w_hi[:, cols].bitcast(F32), ALU.subtract)\
                    .then_inc(w_lo_mlp_done, 1)

            def stage_x(g, m, more):
                for t in range(TILES):
                    y_bias(m, t)
                    if t > 0:
                        x1_power(g, t - 1)
                    if more and t == 3:
                        x_power(g + 1)
                    if t + 2 < TILES:
                        k_diagonal(g, t + 2)
                    if t + 1 < TILES:
                        subtract_max(g, t + 1)
                    g_second(m, 2 * t + 1)

            def stage_x_alone(g):
                k_diagonal(g, 2)
                for t in range(TILES):
                    if t + 1 < TILES:
                        subtract_max(g, t + 1)
                    if t > 0:
                        x1_power(g, t - 1)
                    if t == 0:
                        k_diagonal(g, 3)
                    if t == 3:
                        x_power(g + 1)
                    for s in range(2 + 2 * t, min(4 + 2 * t, W_CHUNKS)):
                        w_split_lo(s)

            def stage_y(g, more):
                x1_power(g, TILES - 1)
                if more:
                    k_diagonal(g + 1, 0)
                    k_diagonal(g + 1, 1)
                    x_bias(g + 1)
                    subtract_max(g + 1, 0)

            pool.wait_ge(consts_ready, 1)
            x_power(0)
            pool.wait_ge(rows_loaded, 16)
            x_bias(0)
            pool.wait_ge(kdiag_built, 2)
            k_diagonal(0, 1)
            subtract_max(0, 0)
            stage_x_alone(0)
            stage_y(0, True)
            with pool.Fori(1, GROUPS - 1) as g:
                stage_x(g, g - 1, True)
                stage_y(g, True)
            last = GROUPS - 1
            stage_x(last, last - 1, False)
            stage_y(last, False)
            for t in range(TILES):
                y_bias(last, t)
            for j in range(1, FJ, 2):
                g_second(last, j)

        @block.vector
        def _(dve):
            dve.memset(v_diag[:], 0.0).then_inc(mask_step, 1)
            dve.wait_ge(ident_ready, 2)
            dve.tensor_reduce(head_rows[:], ident[:].rearrange("p (h d) -> p h d", d=D), AX_X, ALU.add)\
                .then_inc(heads_ready, 1)
            dve.wait_ge(mask_step, 1)
            for hp in range(2):
                for b in range(BT):
                    last = dve.memset(v_diag[hp * SEQ:(hp + 1) * SEQ, :, :, 0, b, hp, D], 1.0)
            last.then_inc(vdiag_ready, 1)

            def masks():
                dve.wait_ge(mask_loaded, 16 * BT)
                dve.tensor_scalar(mask_add[:], mask_raw, 0, None, ALU.is_equal).then_inc(mask_step, 1)
                dve.wait_ge(mask_step, 2)
                dve.tensor_reduce(all_masked[:], mask_add[:], AX_X, ALU.min).then_inc(mask_step, 1)
                dve.wait_ge(mask_step, 3)
                dve.tensor_scalar(score_mul[:], all_masked[:], -SCALE, SCALE, ALU.mult, ALU.add)\
                    .then_inc(mask_step, 1)
                dve.tensor_tensor(mask_add[:], mask_add[:], all_masked[:].unsqueeze(2).broadcast_to([P, NT, SEQ]),
                                  ALU.subtract).then_inc(mask_step, 1)
                dve.wait_ge(mask_step, 5)
                dve.tensor_scalar(mask_add[:], mask_add[:], MASKED, None, ALU.mult).then_inc(mask_step, 1)
                dve.wait_ge(mask_step, 6)

            def w_split(s):
                cols = slice(s * WCH, (s + 1) * WCH)
                dve.wait_ge(w_loaded[s % 2], 16 * (s // 2 + 1))
                dve.tensor_copy(w_hi[:, cols], w_raw[:, s % 2, :]).then_inc(w_hi_done, 1)
                dve.wait_ge(w_hi_done, s + 1)
                dve.tensor_tensor(w_lo[:, cols], w_raw[:, s % 2, :], w_hi[:, cols].bitcast(F32), ALU.subtract)\
                    .then_inc(w_lo_done, 1)

            def cond_silu_():
                dve.wait_ge(cond_tanh_done, 1)
                dve.scalar_tensor_tensor(out=cond[:], in0=cond_tanh[:], scalar=1.0, in1=cond[:], op0=ALU.add,
                                         op1=ALU.mult).then_inc(mod_step, 1)
                dve.wait_ge(mod_step, 1)
                dve.tensor_scalar(cond[:], cond[:], 0.5, None, ALU.mult).then_inc(cond_silu, 1)

            def modulation():
                dve.wait_ge(vec_loaded, 16)
                dve.wait_ge(mod_done, 2)
                for m in range(CK):
                    cols = slice(m * BATCH, (m + 1) * BATCH)
                    dve.tensor_scalar(scale_w[:, m, :], ps_m[:, 0, cols], vec[:, SCALE_B + m:SCALE_B + m + 1], 1.0,
                                      ALU.add, ALU.add).then_inc(mod_step, 1)
                    dve.tensor_scalar(shift[:, m, :], ps_m[:, 1, cols], vec[:, SHIFT_B + m:SHIFT_B + m + 1], None,
                                      ALU.add).then_inc(mod_step, 1)
                dve.wait_ge(mod_step, 2 * CK + 1)
                dve.tensor_scalar(scale_w[:], scale_w[:], 0.1, 10.0, ALU.max, ALU.min).then_inc(mod_step, 1)
                dve.wait_ge(mod_step, 2 * CK + 2)
                for m in range(CK):
                    dve.tensor_scalar(scale_w[:, m, :], scale_w[:, m, :], vec[:, NORM_W + m:NORM_W + m + 1], None,
                                      ALU.mult).then_inc(ps_m_read if m == 0 else mod_step, 1)
                dve.wait_ge(ps_m_read, 1)
                dve.wait_ge(mod_step, 3 * CK + 1)

            def by_seq(table, g, c):
                return table[:, c, bass.ds(BG * g, BG)].unsqueeze(2).broadcast_to([P, BG, SEQ])

            def adaln(g, src, src_done, scaled, full, hi, hi_done, lo, lo_done):
                seqs = lambda ap: ap.rearrange("p (b k) -> p b k", b=BG)
                for c in range(CK):
                    dve.wait_ge(src_done, CK * g + c + 1)
                    dve.tensor_tensor(seqs(h_full[:, c, :]), seqs(src[:, c, :]), by_seq(scale_w, g, c), ALU.mult)\
                        .then_inc(scaled, 1)
                for c in range(CK):
                    dve.wait_ge(scaled, CK * g + c + 1)
                    dve.tensor_tensor(seqs(h_full[:, c, :]), seqs(h_full[:, c, :]), by_seq(shift, g, c), ALU.add)\
                        .then_inc(full, 1)
                for c in range(CK):
                    dve.wait_ge(hi_done, CK * g + c + 1)
                    dve.tensor_tensor(lo[:, c, :], h_full[:, c, :], hi[:, c, :].bitcast(F32), ALU.subtract)\
                        .then_inc(lo_done, 1)

            def adaln1(g):
                if isinstance(g, int) and g < 2:
                    pass
                else:
                    dve.wait_ge(h2_lo_done, CK * (g - 1))
                adaln(g, ps_p, xt_done, h1_scaled, h1_full, h1_hi, h1_hi_done, h1_lo, h1_lo_done)

            def adaln2(g, more):
                if more:
                    dve.wait_ge(h1_lo_done, CK * (g + 2))
                adaln(g, ps_c, x1t_done, h2_scaled, h2_full, h2_hi, h2_hi_done, h2_lo, h2_lo_done)

            flat = lambda i: v_part[:, i].rearrange("p j h d -> p (j h d)")

            def v_second(g, t):
                n = TILES * g + t
                dve.wait_ge(v1_done, n + 1)
                if not is0(n):
                    dve.wait_ge(v3_done, n)
                dve.tensor_tensor(v_rest[:], ps_p[:, 0, 0:C], flat(0), ALU.subtract).then_inc(v_rest_done, 1)

            def v_third(g, t):
                n = TILES * g + t
                dve.wait_ge(v_rest_done, n + 1)
                dve.tensor_copy(flat(1), v_rest[:]).then_inc(v2_done, 1)
                dve.wait_ge(v2_done, n + 1)
                dve.tensor_tensor(flat(2), v_rest[:], flat(1), ALU.subtract).then_inc(v3_done, 1)

            heads = lambda ap: ap.rearrange("p (h k) -> p h k", k=SEQ)

            def scores_masked(g, t):
                n = TILES * g + t
                if isinstance(n, int) and n < 2:
                    pass
                else:
                    dve.wait_ge(pt_done, 2 * n - 2)
                for c in range(CK):
                    dve.wait_ge(s_done, 2 * n + c + 1)
                    dve.scalar_tensor_tensor(out=heads(s_sb[:, t % 2, c * 512:(c + 1) * 512]),
                                             in0=heads(ps_s[:, c, :]), scalar=score_mul[:, bass.ds(n, 1)],
                                             in1=mask_add[:, bass.ds(n, 1), :].broadcast_to([P, HC, SEQ]),
                                             op0=ALU.mult, op1=ALU.add).then_inc(s_masked, 1)

            def scores_max(g, t):
                n = TILES * g + t
                dve.wait_ge(s_masked, 2 * n + 2)
                dve.tensor_reduce(s_max[:, t % 2, :], heads(s_sb[:, t % 2, :]), AX_X, ALU.max).then_inc(max_done, 1)

            def p_second(g, t):
                n = TILES * g + t
                if not is0(n):
                    dve.wait_ge(pv_done, n)
                for half in range(2):
                    dve.wait_ge(p_hi_done, 2 * n + half + 1)
                    js = slice(half * 4, half * 4 + 4)
                    dve.tensor_tensor(p_lo[:, js, :].rearrange("p j q -> p (j q)"), ps_p[:, half, :],
                                      p_hi[:, js, :].rearrange("p j q -> p (j q)"), ALU.subtract)\
                        .then_inc(p_lo_done, 1)

            def normalise_o(g, t):
                n = TILES * g + t
                dve.wait_ge(pv_done, n + 1)
                if not is0(n):
                    dve.wait_ge(ot_done, n)
                pv = [ps_c[b * SEQ:(b + 1) * SEQ, :, b * HC * VW:(b + 1) * HC * VW]
                      .rearrange("p c (h d) -> p c h d", d=VW) for b in range(BT)]
                for b in range(BT):
                    dve.reciprocal(sum_inv[b * SEQ:(b + 1) * SEQ], pv[b][:, :, :, D]).then_inc(sum_inverted, 1)
                for b in range(BT):
                    dve.wait_ge(sum_inverted, 2 * n + b + 1)
                    rows_ = slice(b * SEQ, (b + 1) * SEQ)
                    dve.tensor_tensor(o_sb[rows_, :].rearrange("p (c h d) -> p c h d", c=CK, h=HC), pv[b][:, :, :, 0:D],
                                      sum_inv[rows_].unsqueeze(3).broadcast_to([SEQ, CK, HC, D]), ALU.mult)\
                        .then_inc(o_done, 1)

            def o_second(g, t):
                n = TILES * g + t
                dve.wait_ge(o_hi_done, n + 1)
                dve.tensor_tensor(o_lo[:], ps_c[:, 0, 0:C], o_hi[:].bitcast(F32), ALU.subtract)\
                    .then_inc(o_lo_done, 1)

            def x1_add(g, t):
                n = TILES * g + t
                dve.wait_ge(proj_done, n + 1)
                dve.wait_ge(x_biased, n + 1)
                if not is0(g):
                    dve.wait_ge(y_biased, n - TILES + 1)
                dve.tensor_tensor(x1[:, t, :], ps_c[:, 1, 0:C], x_res[:, t, :], ALU.add).then_inc(x1_done, 1)

            def x_clamp(g):
                if not is0(g):
                    dve.wait_ge(x_normed, TILES * g)
                dve.wait_ge(x_powed, g + 1)
                dve.tensor_scalar(x_inv[:], x_pow[:], 1.0 / EPS, None, ALU.min).then_inc(x_inverted, 1)

            def x1_clamp(g, t):
                n = TILES * g + t
                if not is0(g):
                    dve.wait_ge(x1_normed, n - TILES + 1)
                dve.wait_ge(x1_powed, n + 1)
                dve.tensor_scalar(x1_inv[:, t:t + 1], x1_pow[:, t:t + 1], 1.0 / EPS, None, ALU.min)\
                    .then_inc(x1_inverted, 1)

            def gate_up(m, j, bank=ps_m):
                n = FJ * m + j
                dve.wait_ge(up_done, n + 1)
                dve.wait_ge(gate_read, n + 1)
                dve.scalar_tensor_tensor(out=gate[:, j % 2, :], in0=bank[:, 1, :],
                                         scalar=vec[:, MLP_B1 + FJ + j:MLP_B1 + FJ + j + 1], in1=gate[:, j % 2, :],
                                         op0=ALU.add, op1=ALU.mult).then_inc(up_read, 1)

            def gated(m, j):
                n = FJ * m + j
                dve.wait_ge(up_read, n + 1)
                dve.scalar_tensor_tensor(out=gate[:, j % 2, :], in0=gate_tanh[:, j % 2, :], scalar=1.0,
                                         in1=gate[:, j % 2, :], op0=ALU.add, op1=ALU.mult).then_inc(g_done, 1)

            def g_second(m, j):
                dve.wait_ge(g_hi_done, FJ * m + j + 1)
                dve.tensor_tensor(g_lo[:, j, :], gate[:, j % 2, :], g_hi[:, j, :].bitcast(F32), ALU.subtract)\
                    .then_inc(g_lo_even, 1)

            def y_add(m, t):
                n = TILES * m + t
                dve.wait_ge(down_done, n + 1)
                dve.wait_ge(y_biased, n + 1)
                dve.tensor_tensor(y[:, t, :], ps_m[:, t % 2, 0:C], y[:, t, :], ALU.add).then_inc(ps_m_read, 1)

            def stage_x(g, m, more):
                for t in range(TILES):
                    if 0 < t < TILES - 1:
                        v_second(g, t + 1)
                    if t > 0:
                        x1_add(g, t - 1)
                    if t + 1 < TILES:
                        scores_masked(g, t + 1)
                        v_third(g, t + 1)
                    p_second(g, t)
                    gate_up(m, 2 * t)
                    if t + 1 < TILES:
                        scores_max(g, t + 1)
                    if t > 0:
                        x1_clamp(g, t - 1)
                    if more and t == 3:
                        x_clamp(g + 1)
                    gated(m, 2 * t)
                    normalise_o(g, t)
                    if t >= 2:
                        o_second(g, t)
                    g_second(m, 2 * t)
                    gate_up(m, 2 * t + 1)
                    gated(m, 2 * t + 1)
                    if t < 2:
                        o_second(g, t)

            def stage_x_alone(g):
                for t in range(TILES):
                    if t > 0:
                        x1_add(g, t - 1)
                    if t + 1 < TILES:
                        scores_masked(g, t + 1)
                        scores_max(g, t + 1)
                    p_second(g, t)
                    if 0 < t < TILES - 1:
                        v_second(g, t + 1)
                    if t + 1 < TILES:
                        v_third(g, t + 1)
                    if t > 0:
                        x1_clamp(g, t - 1)
                    if t == 3:
                        x_clamp(g + 1)
                    normalise_o(g, t)
                    o_second(g, t)

            def stage_y(g, m, more):
                x1_add(g, TILES - 1)
                if more:
                    adaln1(g + 1)
                x1_clamp(g, TILES - 1)
                if m is not None:
                    y_add(m, 0)
                    y_add(m, 1)
                adaln2(g, more)
                if m is not None:
                    y_add(m, 2)
                if more:
                    v_second(g + 1, 0)
                    v_third(g + 1, 0)
                    scores_masked(g + 1, 0)
                    scores_max(g + 1, 0)
                if m is not None:
                    y_add(m, 3)
                if more:
                    v_second(g + 1, 1)

            cond_silu_()
            w_split(0)
            x_clamp(0)
            modulation()
            adaln1(0)
            w_split(1)
            masks()
            for c in range(CK):
                dve.wait_ge(k_copied, c + 1)
                dve.tensor_tensor(k_diag[:, 0, c].rearrange("p b (h k) -> p b h k", h=HC),
                                  k_t[:, c, 0:P].rearrange("p (b k) -> p b k", b=BT).unsqueeze(2)
                                  .broadcast_to([P, BT, HC, SEQ]),
                                  head_rows[:].unsqueeze(1).unsqueeze(3).broadcast_to([P, BT, HC, SEQ]), ALU.mult)\
                    .then_inc(kdiag_built, 1)
            v_second(0, 0)
            v_third(0, 0)
            scores_masked(0, 0)
            scores_max(0, 0)
            v_second(0, 1)
            dve.tensor_scalar(half_b1[:], vec[:, MLP_B1:MLP_B1 + FJ], 0.5, None, ALU.mult).then_inc(half_b1_ready, 1)
            stage_x_alone(0)
            stage_y(0, None, True)
            with dve.Fori(1, GROUPS - 1) as g:
                stage_x(g, g - 1, True)
                stage_y(g, g - 1, True)
            last = GROUPS - 1
            stage_x(last, last - 1, False)
            stage_y(last, last - 1, False)
            for j in range(FJ):
                gate_up(last, j, (ps_m, ps_s)[j % 2])
                gated(last, j)
                if j % 2 == 0:
                    g_second(last, j)
            for t in range(TILES):
                y_add(last, t)


def kernel(x, cond_1024, mask_BxS_ik0, L0_cond_norm_w, L0_cond_scale_w, L0_cond_scale_b, L0_cond_shift_w,
           L0_cond_shift_b, L0_cond_qkv_w, L0_cond_proj_w, L0_cond_proj_b, L0_cond_mlp_w1, L0_cond_mlp_b1,
           L0_cond_mlp_w2, L0_cond_mlp_b2):
    import numpy as np
    import concourse.bacc as bacc
    from concourse.bass_utils import run_bass_kernel_spmd

    def by_input(w):
        w = np.asarray(w)
        return w.T.reshape(-1, P, w.shape[0]).transpose(1, 0, 2).reshape(P, -1)

    def columns(v):
        return np.asarray(v).reshape(-1, P).T

    qkv = np.asarray(L0_cond_qkv_w)
    arrays = {
        "x": np.asarray(x).reshape(BATCH * SEQ, C),
        "cond_t": np.asarray(cond_1024).T.reshape(CK, P, BATCH).transpose(1, 0, 2),
        "mask": np.asarray(mask_BxS_ik0),
        "weights": np.concatenate([by_input(qkv[:2 * C]), by_input(qkv[2 * C:]), by_input(L0_cond_proj_w),
                                   by_input(L0_cond_mlp_w1), by_input(L0_cond_mlp_w2)], axis=1),
        "mod_w": np.stack([by_input(L0_cond_scale_w), by_input(L0_cond_shift_w)], axis=1).reshape(P, 2, CK, C),
        "vecs": np.concatenate([columns(v) for v in (L0_cond_scale_b, L0_cond_shift_b, L0_cond_norm_w,
                                                     L0_cond_mlp_b1)], axis=1),
        "rows": np.stack([np.asarray(L0_cond_proj_b), np.asarray(L0_cond_mlp_b2)]),
    }
    nc = bacc.Bacc("TRN2", target_bir_lowering=False, num_devices=1)
    args = {}
    for name, a in arrays.items():
        arrays[name] = np.ascontiguousarray(a)
        args[name] = nc.dram_tensor(name, a.shape, mybir.dt.from_np(a.dtype), kind="ExternalInput").ap()
    args["out"] = nc.dram_tensor("out", (BATCH * SEQ, C), F32, kind="ExternalOutput").ap()
    block_kernel(nc, **args)
    r = run_bass_kernel_spmd(nc, [arrays], core_ids=[0])
    return r.results[0]["out"].reshape(BATCH, SEQ, C)
```

```python
from contextlib import ExitStack

import concourse.bass as bass
from concourse import mybir

F32 = mybir.dt.float32
F32R = mybir.dt.float32r
BF16 = mybir.dt.bfloat16
F16 = mybir.dt.float16
I32 = mybir.dt.int32
ALU = mybir.AluOpType
ACT = mybir.ActivationFunctionType
AX_X = mybir.AxisListType.X

P = 128
BATCH, SEQ, C = 32, 64, 256
HEADS = 16
D = C // HEADS
F = 4 * C
TILES = 4
GTOK = TILES * P
GROUPS = BATCH * SEQ // GTOK
BT = P // SEQ
BG = TILES * BT
NT = GROUPS * TILES
CK = C // P
HC = HEADS // CK
FJ = F // P
PAIRS = HEADS // 2
SCALE = float(D) ** -0.5
EPS = 1e-6
MASKED = -1.0e30
EXP_SHIFT = 9.7
DOWN_LAG = 3
VW = D + 1

WCH = 1024
QK_AT, V_AT = 0, CK * 2 * C
PR_AT = V_AT + CK * C
W1_AT = PR_AT + CK * C
W2_AT = W1_AT + CK * 2 * F
W_COLS = W2_AT + FJ * C
W_CHUNKS = W_COLS // WCH
W_LO_DVE = (7,)
SCALE_B, SHIFT_B, NORM_W, MLP_B1 = 0, CK, 2 * CK, 3 * CK
VEC_COLS = 3 * CK + 2 * FJ


def block_kernel(nc, x, cond_t, mask, weights, mod_w, vecs, rows, out):
    x_v = x.rearrange("(g t p) c -> g p t c", g=GROUPS, t=TILES)
    out_v = out.rearrange("(n p) c -> n p c", p=P)

    with ExitStack() as ctx:
        def sb(name, shape, dt=F32):
            return ctx.enter_context(nc.sbuf_tensor(name, shape, dt))

        def ps(name, shape):
            return ctx.enter_context(nc.psum_tensor(name, shape, F32))

        def sem(name):
            return ctx.enter_context(nc.semaphore(name))

        w_hi = sb("w_hi", [P, W_COLS], F32R)
        w_lo = sb("w_lo", [P, W_COLS], F32R)
        w_raw = sb("w_raw", [P, 2, WCH])
        vec = sb("vec", [P, VEC_COLS])
        proj_b = sb("proj_b", [P, C])
        mlp_b2 = sb("mlp_b2", [P, C])
        ident = sb("ident", [P, P])
        head_rows = sb("head_rows", [P, HC])
        exp_shift = sb("exp_shift", [P, 1])
        neg_half = sb("neg_half", [P, TILES])
        cond = sb("cond", [P, CK, BATCH])
        scale_w = sb("scale_w", [P, CK, BATCH])
        shift = sb("shift", [P, CK, BATCH])
        mask_add = sb("mask_add", [P, NT, SEQ])
        all_masked = sb("all_masked", [P, NT])
        score_mul = sb("score_mul", [P, NT])
        x_in = sb("x_in", [P, TILES, C])
        x_nrm = sb("x_nrm", [P, TILES, C])
        x_res = sb("x_res", [P, TILES, C])
        x_ssq = sb("x_ssq", [P, TILES])
        x_pow = sb("x_pow", [P, TILES])
        x_inv = sb("x_inv", [P, TILES])
        x1 = sb("x1", [P, TILES, C])
        x1_nrm = sb("x1_nrm", [P, TILES, C])
        x1_ssq = sb("x1_ssq", [P, TILES])
        x1_pow = sb("x1_pow", [P, TILES])
        x1_inv = sb("x1_inv", [P, TILES])
        y = sb("y", [P, TILES, C])
        h_full = sb("h_full", [P, CK, GTOK])
        h1_hi = sb("h1_hi", [P, CK, GTOK], F32R)
        h1_lo = sb("h1_lo", [P, CK, GTOK], F32R)
        h2_hi = sb("h2_hi", [P, CK, GTOK], F32R)
        h2_lo = sb("h2_lo", [P, CK, GTOK], F32R)
        q_t = sb("q_t", [P, CK, GTOK])
        k_t = sb("k_t", [P, CK, GTOK])
        k_diag = sb("k_diag", [P, 2, CK, BT, HC * SEQ])
        s_sb = sb("s_sb", [P, 2, HEADS * SEQ])
        s_max = sb("s_max", [P, 2, HEADS])
        p_hi = sb("p_hi", [P, PAIRS, P], F16)
        p_lo = sb("p_lo", [P, PAIRS, P], F16)
        v_part = sb("v_part", [P, 3, PAIRS, 2, D], BF16)
        v_rest = sb("v_rest", [P, C])
        v_diag = sb("v_diag", [P, 2, PAIRS, 3, BT, 2, VW], BF16)
        sum_inv = sb("sum_inv", [P, 2, HC])
        o_sb = sb("o_sb", [P, C])
        o_hi = sb("o_hi", [P, C], F32R)
        o_lo = sb("o_lo", [P, C], F32R)
        gate = sb("gate", [P, 2, GTOK])
        half_b1 = sb("half_b1", [P, FJ])
        g_hi = sb("g_hi", [P, FJ, GTOK], F32R)
        g_lo = sb("g_lo", [P, FJ, GTOK], F32R)
        gate_tanh = w_raw[:, :, 0:GTOK]
        cond_tanh = y[:, 0, 0:CK * BATCH].rearrange("p (k b) -> p k b", k=CK)
        table_warm = y[:, 1, 0:1]
        mask_raw = s_sb[:, 0, :].bitcast(I32).rearrange("p (n k) -> p n k", k=SEQ)
        mod_sb = s_sb[:, 1, :].rearrange("p (s k n) -> p s k n", s=2, k=CK)

        ps_s = ps("ps_s", [P, 2, 512])
        ps_p = ps("ps_p", [P, 2, 512])
        ps_c = ps("ps_c", [P, 2, 512])
        ps_m = ps("ps_m", [P, 2, 512])

        wqk = [w[:, QK_AT:V_AT].rearrange("p (k n) -> p k n", k=CK) for w in (w_hi, w_lo)]
        wv = [w[:, V_AT:PR_AT].rearrange("p (k n) -> p k n", k=CK) for w in (w_hi, w_lo)]
        wpr = [w[:, PR_AT:W1_AT].rearrange("p (k n) -> p k n", k=CK) for w in (w_hi, w_lo)]
        w1 = [w[:, W1_AT:W2_AT].rearrange("p (k n) -> p k n", k=CK) for w in (w_hi, w_lo)]
        w2 = [w[:, W2_AT:W_COLS].rearrange("p (j n) -> p j n", j=FJ) for w in (w_hi, w_lo)]
        h1, h2, o_t, g_t = (h1_hi, h1_lo), (h2_hi, h2_lo), (o_hi, o_lo), (g_hi, g_lo)
        PARTS = ((0, 0), (0, 1), (1, 0))

        vec_loaded, rows_loaded, cond_loaded = sem("vec_loaded"), sem("rows_loaded"), sem("cond_loaded")
        mask_loaded, mod_loaded = sem("mask_loaded"), sem("mod_loaded")
        w_loaded = [sem("w_loaded_even"), sem("w_loaded_odd")]
        w_hi_done = sem("w_hi_done")
        w_lo_dve, w_lo_pool = sem("w_lo_dve"), sem("w_lo_pool")
        ident_ready, consts_ready = sem("ident_ready"), sem("consts_ready")
        vdiag_ready, mask_step, mod_step = sem("vdiag_ready"), sem("mask_step"), sem("mod_step")
        cond_silu, mod_done, heads_ready = sem("cond_silu"), sem("mod_done"), sem("heads_ready")
        half_b1_ready, cond_tanh_done = sem("half_b1_ready"), sem("cond_tanh_done")
        x_loaded, x_squared, x_powed = sem("x_loaded"), sem("x_squared"), sem("x_powed")
        x_inverted, x_normed, x_biased = sem("x_inverted"), sem("x_normed"), sem("x_biased")
        xt_done, h1_scaled, h1_full = sem("xt_done"), sem("h1_scaled"), sem("h1_full")
        h1_hi_done, h1_lo_done = sem("h1_hi_done"), sem("h1_lo_done")
        k_done, k_copied, q_done, q_copied = sem("k_done"), sem("k_copied"), sem("q_done"), sem("q_copied")
        kdiag_first = sem("kdiag_first")
        kdiag_built, s_done, s_masked = sem("kdiag_built"), sem("s_done"), sem("s_masked")
        max_done, max_subtracted, exp_done = sem("max_done"), sem("max_subtracted"), sem("exp_done")
        pt_done, p_hi_done, p_lo_done = sem("pt_done"), sem("p_hi_done"), sem("p_lo_done")
        v_done, v1_done, v_rest_done = sem("v_done"), sem("v1_done"), sem("v_rest_done")
        v2_done, v3_done, vdiag_built = sem("v2_done"), sem("v3_done"), sem("vdiag_built")
        pv_done, sum_inverted, o_done = sem("pv_done"), sem("sum_inverted"), sem("o_done")
        ot_done, o_hi_done, o_lo_done = sem("ot_done"), sem("o_hi_done"), sem("o_lo_done")
        proj_done, x1_done = sem("proj_done"), sem("x1_done")
        x1_squared, x1_powed, x1_inverted = sem("x1_squared"), sem("x1_powed"), sem("x1_inverted")
        x1_normed, y_biased = sem("x1_normed"), sem("y_biased")
        x1t_done, h2_scaled, h2_full = sem("x1t_done"), sem("h2_scaled"), sem("h2_full")
        h2_hi_done, h2_lo_done = sem("h2_hi_done"), sem("h2_lo_done")
        gate_done, up_done, gate_read = sem("gate_done"), sem("up_done"), sem("gate_read")
        up_read, g_done, g_hi_done = sem("up_read"), sem("g_done"), sem("g_hi_done")
        g_lo_even, g_lo_odd = sem("g_lo_even"), sem("g_lo_odd")
        down_done = sem("down_done")
        ps_m_read = sem("ps_m_read")
        y_free = sem("y_free")

        block = ctx.enter_context(nc.Block())
        is0 = lambda g: isinstance(g, int) and g == 0

        def wait_w_lo(eng, s):
            if s in W_LO_DVE:
                eng.wait_ge(w_lo_dve, W_LO_DVE.index(s) + 1)
            else:
                eng.wait_ge(w_lo_pool, s + 1 - sum(v <= s for v in W_LO_DVE))

        def kdiag_wait(eng, n, c):
            if is0(n):
                eng.wait_ge(kdiag_first, c + 1)
            else:
                eng.wait_ge(kdiag_built, 2 * n + c - 1)

        last_banks = [ps_p[:, 0, 0:C], ps_p[:, 1, 0:C], ps_c[:, 0, 0:C], ps_c[:, 1, 0:C]]

        def v_bank(g, t):
            return ps_m[:, t % 2, 0:C] if is0(g) else ps_p[:, 0, 0:C]

        @block.sync
        def _(sp):
            def load_x(g):
                if not is0(g):
                    sp.wait_ge(x_normed, TILES * g)
                    sp.wait_ge(x_biased, TILES * g)
                src = x_v[g] if isinstance(g, int) else x_v[bass.ds(g, 1)].rearrange("a p t c -> (a p) t c")
                sp.dma_start(x_in[:], src).then_inc(x_loaded, 16)

            def load_w(s):
                if s >= 2:
                    wait_w_lo(sp, s - 2)
                sp.dma_start(w_raw[:, s % 2, :], weights[:, s * WCH:(s + 1) * WCH]).then_inc(w_loaded[s % 2], 16)

            load_x(0)
            sp.dma_start(vec[:], vecs).then_inc(vec_loaded, 16)
            load_w(0)
            load_w(1)
            sp.dma_start(proj_b[:], rows[0:1, :].broadcast_to([P, C])).then_inc(rows_loaded, 16)
            for b in range(BT):
                src = mask.rearrange("(n b) k -> b n k", b=BT)[b:b + 1].broadcast_to([SEQ, NT, SEQ])
                sp.dma_start(mask_raw[b * SEQ:(b + 1) * SEQ], src).then_inc(mask_loaded, 16)
            sp.dma_start(mlp_b2[:], rows[1:2, :].broadcast_to([P, C])).then_inc(y_free, 16)
            for s in range(2, 4):
                load_w(s)
            load_x(1)
            for s in range(4, W_CHUNKS):
                load_w(s)

            def store_y(g):
                for t in range(TILES):
                    n = TILES * g + t
                    sp.wait_ge(ps_m_read, n + 2)
                    dst = out_v[n] if isinstance(n, int) else out_v[bass.ds(n, 1)].rearrange("a p c -> (a p) c")
                    sp.dma_start(dst, y[:, t, :]).then_inc(y_free, 16)

            with sp.Fori(1, GROUPS - 1) as g:
                load_x(g + 1)
                store_y(g - 1)
            store_y(GROUPS - 2)
            store_y(GROUPS - 1)
            sp.wait_ge(y_free, 16 * NT + 16)

        @block.tensor
        def _(pe):
            def product(dst, lhs, rhs, lhs_at, rhs_at, n):
                for k in range(n):
                    for a, b in PARTS:
                        last = pe.matmul(dst, lhs[a][:, k, lhs_at], rhs[b][:, k, rhs_at],
                                         start=(k == 0 and (a, b) == PARTS[0]),
                                         stop=(k == n - 1 and (a, b) == PARTS[-1]))
                return last

            def keep_warm(n, bank=ps_c):
                for _ in range(n):
                    pe.matmul(bank[:, 1, 3 * P:4 * P], ident[:], ident[:], start=True, stop=True)

            def modulation():
                pe.wait_ge(cond_silu, 1)
                pe.wait_ge(mod_loaded, 16)
                for s in range(2):
                    for m in range(CK):
                        for k in range(CK):
                            last = pe.matmul(ps_m[:, s, m * BATCH:(m + 1) * BATCH],
                                             mod_sb[:, s, k, m * P:(m + 1) * P], cond[:, k, :],
                                             start=(k == 0), stop=(k == CK - 1))
                    last.then_inc(mod_done, 1)

            def x_transposed(g, bank=ps_p):
                if bank is ps_m:
                    pe.wait_ge(v_rest_done, TILES)
                elif not is0(g):
                    pe.wait_ge(p_lo_done, 2 * TILES * g)
                for t in range(TILES):
                    pe.wait_ge(x_normed, TILES * g + t + 1)
                    for c in range(CK):
                        last = pe.transpose(bank[:, c, t * P:(t + 1) * P], x_nrm[:, t, c * P:(c + 1) * P], ident[:])
                        if t == TILES - 1:
                            last.then_inc(xt_done, 1)

            def k_proj(g, chunks=range(CK)):
                pe.wait_ge(h1_lo_done, CK * g + CK)
                for c in chunks:
                    if not is0(g):
                        pe.wait_ge(s_masked, 2 * TILES * g - 1 + c)
                    product(ps_s[:, c, :], wqk, h1, slice(C + c * P, C + (c + 1) * P), slice(0, GTOK), CK)\
                        .then_inc(k_done, 1)

            def q_proj(g):
                for c in range(CK):
                    pe.wait_ge(k_copied, CK * g + c + 1)
                    product(ps_s[:, c, :], wqk, h1, slice(c * P, (c + 1) * P), slice(0, GTOK), CK)\
                        .then_inc(q_done, 1)

            def v_proj(g, t):
                n = TILES * g + t
                if is0(g) and t < 2:
                    pe.wait_ge(ps_m_read, 1)
                elif is0(g):
                    pe.wait_ge(v_rest_done, t - 1)
                elif t == 0:
                    pe.wait_ge(h1_scaled, CK * g + CK)
                    pe.wait_ge(p_lo_done, 2 * TILES * g)
                elif t == 1:
                    pe.wait_ge(v_rest_done, n)
                else:
                    pe.wait_ge(p_lo_done, 2 * (n - 2) + 1)
                product(v_bank(g, t), h1, wv, slice(t * P, (t + 1) * P), slice(0, C), CK).then_inc(v_done, 1)

            def scores(g, t):
                n = TILES * g + t
                pe.wait_ge(q_copied, CK * g + CK)
                for c in range(CK):
                    kdiag_wait(pe, n, c)
                    if t > 0:
                        pe.wait_ge(s_masked, 2 * n - 1 + c)
                    for b in range(BT):
                        last = pe.matmul(ps_s[b * SEQ:(b + 1) * SEQ, c, :],
                                         q_t[:, c, t * P + b * SEQ:t * P + (b + 1) * SEQ],
                                         k_diag[:, t % 2, c, b, :], start=True, stop=True)
                    last.then_inc(s_done, 1)

            def p_transposed(g, t):
                n = TILES * g + t
                pe.wait_ge(exp_done, n + 1)
                if not is0(g):
                    pe.wait_ge(v_rest_done, TILES * g + min(t + 2, TILES))
                elif t == 0:
                    pe.wait_ge(h1_scaled, CK)
                if t > 0:
                    pe.wait_ge(p_lo_done, 2 * n)
                for half in range(2):
                    for j in range(4):
                        at = (half * 4 + j) * P
                        last = pe.transpose(ps_p[:, half, j * P:(j + 1) * P], s_sb[:, t % 2, at:at + P], ident[:])
                    last.then_inc(pt_done, 1)

            def p_times_v(g, t):
                n = TILES * g + t
                pe.wait_ge(vdiag_built, 4 * n + 4)
                if t > 0:
                    pe.wait_ge(o_lo_done, n)
                    pe.wait_ge(x1_done, n)
                elif not is0(g):
                    pe.wait_ge(h2_scaled, CK * g)
                for half in range(2):
                    pe.wait_ge(p_lo_done, 2 * n + half + 1)
                    for j in range(4):
                        pair = half * 4 + j
                        dst = ps_c[:, half, 0:BT * 4 * 2 * VW]\
                            .rearrange("p (b j n) -> p b j n", b=BT, j=4)[:, :, j, :]
                        terms = [(p_hi, 0), (p_hi, 1), (p_hi, 2), (p_lo, 0), (p_lo, 1)]
                        for i, (part, v) in enumerate(terms):
                            last = pe.matmul(dst, part[:, pair, :],
                                             v_diag[:, t % 2, pair, v].rearrange("p b h n -> p b (h n)"),
                                             start=(i == 0), stop=(i == len(terms) - 1))
                last.then_inc(pv_done, 1)

            def o_transposed(g, t):
                pe.wait_ge(o_done, 2 * (TILES * g + t) + 2)
                for c in range(CK):
                    last = pe.transpose(ps_c[:, 0, c * P:(c + 1) * P], o_sb[:, c * P:(c + 1) * P], ident[:])
                last.then_inc(ot_done, 1)

            def projection(g, t):
                pe.wait_ge(o_lo_done, TILES * g + t + 1)
                o_v = [o[:, :].rearrange("p (k n) -> p k n", k=CK) for o in o_t]
                product(ps_c[:, 1, 0:C], o_v, wpr, slice(0, P), slice(0, C), CK).then_inc(proj_done, 1)

            def x1_transposed(g):
                pe.wait_ge(x1_normed, TILES * g + TILES)
                pe.wait_ge(o_lo_done, TILES * g + TILES)
                pe.wait_ge(x1_done, TILES * g + TILES)
                for c in range(CK):
                    for t in range(TILES):
                        last = pe.transpose(ps_c[:, c, t * P:(t + 1) * P], x1_nrm[:, t, c * P:(c + 1) * P], ident[:])
                    last.then_inc(x1t_done, 1)

            def mlp_gate(m, j, bank=ps_m, ahead=0):
                n = FJ * m + j
                if j == 0:
                    pe.wait_ge(h2_lo_done, CK * m + CK)
                if j <= ahead and bank is ps_m:
                    pe.wait_ge(ps_m_read, TILES * m + 1)
                elif j > ahead:
                    pe.wait_ge(gate_read, n - ahead)
                product(bank[:, 0, :], w1, h2, slice(j * P, (j + 1) * P), slice(0, GTOK), CK).then_inc(gate_done, 1)

            def mlp_up(m, j, bank=ps_m, ahead=0):
                n = FJ * m + j
                if j > ahead:
                    pe.wait_ge(up_read, n - ahead)
                product(bank[:, 1, :], w1, h2, slice(F + j * P, F + (j + 1) * P), slice(0, GTOK), CK)\
                    .then_inc(up_done, 1)

            def mlp_down(m, t, js=range(FJ)):
                n = TILES * m + t
                if js[0] == 0:
                    if t == 0:
                        pe.wait_ge(gate_read, FJ * m + FJ)
                    elif t == 1:
                        pe.wait_ge(up_read, FJ * m + FJ)
                    else:
                        pe.wait_ge(ps_m_read, n)
                for j in js:
                    if t == 0:
                        wait_g(m, j)
                    last = down_chunk(m, t, j, ps_m[:, t % 2, 0:C])
                if js[-1] == FJ - 1:
                    last.then_inc(down_done, 1)

            def wait_g(m, j):
                pe.wait_ge((g_lo_even, g_lo_odd)[j % 2], FJ // 2 * m + j // 2 + 1)

            def down_chunk(m, t, j, dst):
                for a, b in PARTS:
                    last = pe.matmul(dst, g_t[a][:, j, t * P:(t + 1) * P], w2[b][:, j, :],
                                     start=(j == 0 and (a, b) == PARTS[0]), stop=(j == FJ - 1 and (a, b) == PARTS[-1]))
                return last

            def last_mlp(m):
                for step in range(FJ + DOWN_LAG):
                    if step < FJ:
                        mlp_gate(m, step, (ps_s, ps_m)[step % 2], 1)
                        mlp_up(m, step, (ps_s, ps_m)[step % 2], 1)
                    j = step - DOWN_LAG
                    if j >= 0:
                        wait_g(m, j)
                        for t in range(TILES):
                            last = down_chunk(m, t, j, last_banks[t])
                            if j == FJ - 1:
                                last.then_inc(down_done, 1)

            def early(more):
                return 2 if more else 6

            def stage_x(g, m, more):
                for t in range(TILES):
                    if t < TILES - 1:
                        mlp_gate(m, 2 * t)
                    p_transposed(g, t)
                    mlp_up(m, 2 * t)
                    mlp_gate(m, 2 * t + 1)
                    p_times_v(g, t)
                    mlp_up(m, 2 * t + 1)
                    if t + 2 < TILES:
                        v_proj(g, t + 2)
                    o_transposed(g, t)
                    if t + 2 < TILES:
                        scores(g, t + 2)
                    if t == 2:
                        mlp_gate(m, 6)
                    if more and t == 3:
                        x_transposed(g + 1)
                    if t == 3:
                        mlp_down(m, 0, range(early(more)))
                    projection(g, t)

            def first_group():
                v_proj(0, 2)
                keep_warm(7)
                p_transposed(0, 0)
                for t in range(TILES):
                    if t == 1:
                        v_proj(0, 3)
                    if t == 2:
                        x_transposed(1, ps_m)
                    p_times_v(0, t)
                    if t + 2 < TILES:
                        scores(0, t + 2)
                    if t == 2:
                        keep_warm(5, ps_p)
                    if t == 3:
                        k_proj(1, (0,))
                    o_transposed(0, t)
                    if t == 2:
                        keep_warm(5, ps_p)
                    if t + 1 < TILES:
                        p_transposed(0, t + 1)
                    else:
                        v_proj(1, 0)
                        k_proj(1, (1,))
                    projection(0, t)
                    if t == 2:
                        pe.wait_ge(h1_scaled, 2 * CK)
                        keep_warm(4, ps_m)
                q_proj(1)
                x1_transposed(0)
                scores(1, 0)
                v_proj(1, 1)
                scores(1, 1)
                keep_warm(3, ps_m)

            def stage_y(g, m, more):
                if more:
                    mlp_down(m, 0, range(early(more), FJ))
                    mlp_down(m, 1)
                    k_proj(g + 1)
                    x1_transposed(g)
                else:
                    mlp_down(m, 1, range(early(more)))
                    mlp_down(m, 0, range(early(more), FJ))
                    x1_transposed(g)
                    mlp_down(m, 1, range(early(more), FJ))
                if more:
                    q_proj(g + 1)
                mlp_down(m, 2)
                if more:
                    v_proj(g + 1, 0)
                    scores(g + 1, 0)
                mlp_down(m, 3)
                if more:
                    v_proj(g + 1, 1)
                    scores(g + 1, 1)

            pe.wait_ge(ident_ready, 2)
            keep_warm(10)
            modulation()
            x_transposed(0)
            keep_warm(12)
            wait_w_lo(pe, 0)
            k_proj(0)
            wait_w_lo(pe, 1)
            v_proj(0, 0)
            q_proj(0)
            v_proj(0, 1)
            scores(0, 0)
            scores(0, 1)
            pe.wait_ge(vdiag_ready, 1)
            first_group()
            wait_w_lo(pe, W_CHUNKS - 1)
            wait_w_lo(pe, W_CHUNKS - 2)
            with pe.Fori(1, GROUPS - 1) as g:
                stage_x(g, g - 1, True)
                stage_y(g, g - 1, True)
            last = GROUPS - 1
            stage_x(last, last - 1, False)
            stage_y(last, last - 1, False)
            last_mlp(last)

        @block.scalar
        def _(act):
            act.dma_start(cond[:], cond_t).then_inc(cond_loaded, 16)
            act.dma_start(mod_sb, mod_w).then_inc(mod_loaded, 16)
            act.wait_ge(consts_ready, 2)
            act.activation(table_warm[:], exp_shift[:], ACT.Exp)
            act.wait_ge(cond_loaded, 16)
            act.activation(cond_tanh[:], cond[:], ACT.Tanh, scale=0.5).then_inc(cond_tanh_done, 1)

            def w_split_hi(s):
                act.wait_ge(w_loaded[s % 2], 16 * (s // 2 + 1))
                act.activation(w_hi[:, s * WCH:(s + 1) * WCH], w_raw[:, s % 2, :], ACT.Copy)\
                    .then_inc(w_hi_done, 1)

            def x_squares(g):
                act.wait_ge(x_loaded, 16 * g + 16)
                if not is0(g):
                    act.wait_ge(xt_done, CK * g)
                    act.wait_ge(x_inverted, g)
                for t in range(TILES):
                    act.activation(x_nrm[:, t, :], x_in[:, t, :], ACT.Square, scale=1.0 / 16.0,
                                   accum_out=x_ssq[:, t:t + 1]).then_inc(x_squared, 1)

            def x_norms(g, tiles=range(TILES)):
                act.wait_ge(x_inverted, g + 1)
                act.wait_ge(x_squared, TILES * g + TILES)
                for t in tiles:
                    act.activation(x_nrm[:, t, :], x_in[:, t, :], ACT.Copy, scale=x_inv[:, t:t + 1])\
                        .then_inc(x_normed, 1)

            def h1_parts(g):
                if not is0(g):
                    act.wait_ge(v_done, TILES * g)
                for c in range(CK):
                    act.wait_ge(h1_full, CK * g + c + 1)
                    act.activation(h1_hi[:, c, :], h_full[:, c, :], ACT.Copy).then_inc(h1_hi_done, 1)

            def h2_parts(g):
                if not is0(g):
                    act.wait_ge(up_done, FJ * g)
                for c in range(CK):
                    act.wait_ge(h2_full, CK * g + c + 1)
                    act.activation(h2_hi[:, c, :], h_full[:, c, :], ACT.Copy).then_inc(h2_hi_done, 1)

            def k_copy(g, chunks=range(CK)):
                if not is0(g):
                    kdiag_wait(act, TILES * g - 1, CK - 1)
                for c in chunks:
                    act.wait_ge(k_done, CK * g + c + 1)
                    act.activation(k_t[:, c, :], ps_s[:, c, :], ACT.Copy).then_inc(k_copied, 1)

            def q_copy(g, chunks=range(CK)):
                if not is0(g):
                    act.wait_ge(s_done, 2 * TILES * g)
                for c in chunks:
                    act.wait_ge(q_done, CK * g + c + 1)
                    act.activation(q_t[:, c, :], ps_s[:, c, :], ACT.Copy).then_inc(q_copied, 1)

            def v_first(g, t):
                n = TILES * g + t
                act.wait_ge(v_done, n + 1)
                if not is0(n):
                    act.wait_ge(vdiag_built, 4 * n)
                act.activation(v_part[:, 0].rearrange("p j h d -> p (j h d)"), v_bank(g, t), ACT.Copy)\
                    .then_inc(v1_done, 1)

            def v_placed(g, t):
                n = TILES * g + t
                act.wait_ge(v3_done, n + 1)
                if isinstance(n, int) and n < 2:
                    act.wait_ge(vdiag_ready, 1)
                else:
                    act.wait_ge(pv_done, n - 1)
                for b in range(BT):
                    for hp in range(2):
                        act.activation(v_diag[hp * SEQ:(hp + 1) * SEQ, t % 2, :, :, b, hp, 0:D],
                                       v_part[b * SEQ:(b + 1) * SEQ, :, :, hp, :].rearrange("p i j d -> p j i d"),
                                       ACT.Copy).then_inc(vdiag_built, 1)

            def exps(g, t):
                n = TILES * g + t
                act.wait_ge(max_subtracted, n + 1)
                act.activation(s_sb[:, t % 2, :], s_sb[:, t % 2, :], ACT.Exp, bias=exp_shift[:, 0:1])\
                    .then_inc(exp_done, 1)

            def p_first(g, t):
                n = TILES * g + t
                if not is0(n):
                    act.wait_ge(pv_done, n)
                for half in range(2):
                    act.wait_ge(pt_done, 2 * n + half + 1)
                    act.activation(p_hi[:, half * 4:half * 4 + 4, :].rearrange("p j q -> p (j q)"),
                                   ps_p[:, half, :], ACT.Copy).then_inc(p_hi_done, 1)

            def o_first(g, t):
                n = TILES * g + t
                act.wait_ge(ot_done, n + 1)
                if not is0(n):
                    act.wait_ge(proj_done, n)
                act.activation(o_hi[:], ps_c[:, 0, 0:C], ACT.Copy).then_inc(o_hi_done, 1)

            def x1_squares(g, t):
                n = TILES * g + t
                act.wait_ge(x1_done, n + 1)
                if not is0(g):
                    act.wait_ge(x1t_done, CK * g)
                act.activation(x1_nrm[:, t, :], x1[:, t, :], ACT.Square, scale=1.0 / 16.0,
                               accum_out=x1_ssq[:, t:t + 1]).then_inc(x1_squared, 1)

            def x1_norm(g, t):
                act.wait_ge(x1_inverted, TILES * g + t + 1)
                act.wait_ge(x1_squared, TILES * g + t + 1)
                act.activation(x1_nrm[:, t, :], x1[:, t, :], ACT.Copy, scale=x1_inv[:, t:t + 1])\
                    .then_inc(x1_normed, 1)

            def gate_parts(m, j, bank=ps_m):
                n = FJ * m + j
                act.wait_ge(gate_done, n + 1)
                if j >= 2:
                    act.wait_ge((g_lo_even, g_lo_odd)[j % 2], FJ // 2 * m + j // 2)
                act.activation(gate_tanh[:, j % 2, :], bank[:, 0, :], ACT.Tanh, bias=half_b1[:, j:j + 1], scale=0.5)
                act.activation(gate[:, j % 2, :], bank[:, 0, :], ACT.Identity, bias=half_b1[:, j:j + 1], scale=0.5)\
                    .then_inc(gate_read, 1)

            def g_first(m, j):
                n = FJ * m + j
                act.wait_ge(g_done, n + 1)
                act.activation(g_hi[:, j, :], gate[:, j % 2, :], ACT.Copy).then_inc(g_hi_done, 1)

            def stage_x(g, m, more):
                for t in range(TILES):
                    gate_parts(m, 2 * t)
                    p_first(g, t)
                    if t == 3:
                        x1_norm(g, 1)
                    if t > 0:
                        x1_squares(g, t - 1)
                    if more and t == 3:
                        x_norms(g + 1)
                    if t + 1 < TILES:
                        v_placed(g, t + 1)
                    gate_parts(m, 2 * t + 1)
                    if t == 3:
                        o_first(g, t)
                    g_first(m, 2 * t)
                    if t + 2 < TILES:
                        v_first(g, t + 2)
                    if t < TILES - 1:
                        o_first(g, t)
                    if t == 1 or t == 3:
                        x1_norm(g, t - 1)
                    if more and t == 1:
                        x_squares(g + 1)
                    if t + 1 < TILES:
                        exps(g, t + 1)
                    g_first(m, 2 * t + 1)

            def first_group():
                p_first(0, 0)
                w_split_hi(4)
                v_placed(0, 1)
                v_first(0, 2)
                exps(0, 1)
                o_first(0, 0)

                p_first(0, 1)
                v_placed(0, 2)
                v_first(0, 3)
                x1_squares(0, 0)
                x_norms(1)
                exps(0, 2)
                o_first(0, 1)

                p_first(0, 2)
                v_placed(0, 3)
                x1_squares(0, 1)
                x1_norm(0, 0)
                w_split_hi(5)
                w_split_hi(6)
                exps(0, 3)
                o_first(0, 2)

                p_first(0, 3)
                h1_parts(1)
                x1_squares(0, 2)
                x1_norm(0, 1)
                w_split_hi(7)
                k_copy(1, (0,))
                o_first(0, 3)
                v_first(1, 0)
                x1_norm(0, 2)
                k_copy(1, (1,))
                x1_squares(0, 3)
                q_copy(1, (0,))
                x1_norm(0, 3)
                q_copy(1, (1,))
                v_placed(1, 0)
                h2_parts(0)
                v_first(1, 1)
                exps(1, 0)

            def stage_y(g, more):
                if more:
                    h1_parts(g + 1)
                x1_squares(g, TILES - 1)
                x1_norm(g, TILES - 1)
                if more:
                    k_copy(g + 1)
                h2_parts(g)
                if more:
                    q_copy(g + 1)
                    v_first(g + 1, 0)
                    v_placed(g + 1, 0)
                    exps(g + 1, 0)
                    v_first(g + 1, 1)

            x_squares(0)
            x_norms(0)
            w_split_hi(0)
            w_split_hi(1)
            h1_parts(0)
            w_split_hi(2)
            k_copy(0)
            v_first(0, 0)
            q_copy(0)
            v_placed(0, 0)
            v_first(0, 1)
            w_split_hi(3)
            x_squares(1)
            exps(0, 0)
            first_group()
            act.wait_ge(half_b1_ready, 1)
            with act.Fori(1, GROUPS - 1) as g:
                stage_x(g, g - 1, True)
                stage_y(g, True)
            last = GROUPS - 1
            stage_x(last, last - 1, False)
            stage_y(last, False)
            for j in range(FJ):
                if j > 0:
                    g_first(last, j - 1)
                gate_parts(last, j, (ps_s, ps_m)[j % 2])
            g_first(last, FJ - 1)

        @block.gpsimd
        def _(pool):
            pool.memset(ident[:], 0.0).then_inc(ident_ready, 1)
            pool.memset(neg_half[:], -0.5).then_inc(consts_ready, 1)
            pool.memset(exp_shift[:], EXP_SHIFT).then_inc(consts_ready, 1)
            pool.wait_ge(ident_ready, 1)
            pool.affine_select(out=ident[:], in_=ident[:], compare_op=ALU.not_equal, fill=1.0, base=0,
                               pattern=[[-1, P]], channel_multiplier=1).then_inc(ident_ready, 1)

            def x_power(g):
                if not is0(g):
                    pool.wait_ge(x_inverted, g)
                pool.wait_ge(x_squared, TILES * g + TILES)
                pool.tensor_tensor(x_pow[:], x_ssq[:], neg_half[:], ALU.pow).then_inc(x_powed, 1)

            def x_bias(g):
                pool.wait_ge(x_loaded, 16 * g + 16)
                if not is0(g):
                    pool.wait_ge(x1_done, TILES * g)
                for t in range(TILES):
                    pool.tensor_tensor(x_res[:, t, :], x_in[:, t, :], proj_b[:], ALU.add).then_inc(x_biased, 1)

            def k_diagonal(g, t, chunks=range(CK)):
                n = TILES * g + t
                for c in chunks:
                    if not isinstance(n, int) or n >= 2:
                        pool.wait_ge(s_done, 2 * n - 3 + c)
                    dst = k_diag[:, t % 2, c].rearrange("p b (h k) -> p b h k", h=HC)
                    src = k_t[:, c, t * P:(t + 1) * P].rearrange("p (b k) -> p b k", b=BT)\
                        .unsqueeze(2).broadcast_to([P, BT, HC, SEQ])
                    of_head = head_rows[:].unsqueeze(1).unsqueeze(3).broadcast_to([P, BT, HC, SEQ])
                    pool.wait_ge(k_copied, CK * g + c + 1)
                    pool.tensor_tensor(dst, src, of_head, ALU.mult).then_inc(kdiag_built, 1)

            def subtract_max(g, t):
                n = TILES * g + t
                pool.wait_ge(max_done, n + 1)
                s_v = s_sb[:, t % 2, :].rearrange("p (h k) -> p h k", h=HEADS)
                pool.tensor_tensor(s_v, s_v, s_max[:, t % 2, :].unsqueeze(2).broadcast_to([P, HEADS, SEQ]),
                                   ALU.subtract).then_inc(max_subtracted, 1)

            def x1_power(g, t):
                n = TILES * g + t
                pool.wait_ge(x1_squared, n + 1)
                if not is0(g):
                    pool.wait_ge(x1_inverted, n - TILES + 1)
                pool.tensor_tensor(x1_pow[:, t:t + 1], x1_ssq[:, t:t + 1], neg_half[:, t:t + 1], ALU.pow)\
                    .then_inc(x1_powed, 1)

            def y_bias(g, t):
                n = TILES * g + t
                pool.wait_ge(x1_done, n + 1)
                pool.wait_ge(y_free, 16 * TILES * g + 16)
                pool.tensor_tensor(y[:, t, :], x1[:, t, :], mlp_b2[:], ALU.add).then_inc(y_biased, 1)

            def g_second(m, j):
                pool.wait_ge(g_hi_done, FJ * m + j + 1)
                pool.tensor_tensor(g_lo[:, j, :], gate[:, j % 2, :], g_hi[:, j, :].bitcast(F32), ALU.subtract)\
                    .then_inc(g_lo_odd, 1)

            def w_split_lo(s):
                pool.wait_ge(w_hi_done, s + 1)
                cols = slice(s * WCH, (s + 1) * WCH)
                pool.tensor_tensor(w_lo[:, cols], w_raw[:, s % 2, :], w_hi[:, cols].bitcast(F32), ALU.subtract)\
                    .then_inc(w_lo_pool, 1)

            def stage_x(g, m, more):
                for t in range(TILES):
                    y_bias(m, t)
                    if t + 2 < TILES:
                        k_diagonal(g, t + 2)
                    if t > 0:
                        x1_power(g, t - 1)
                    if t + 1 < TILES:
                        subtract_max(g, t + 1)
                    if more and t == 1:
                        x_power(g + 1)
                    g_second(m, 2 * t + 1)

            def first_group():
                x_power(1)
                w_split_lo(3)
                w_split_lo(4)
                subtract_max(0, 2)
                x1_power(0, 0)
                subtract_max(0, 3)
                x1_power(0, 1)
                w_split_lo(5)
                w_split_lo(6)
                x1_power(0, 2)
                k_diagonal(1, 0, (0,))
                x1_power(0, 3)
                k_diagonal(1, 0, (1,))
                k_diagonal(1, 1)
                subtract_max(1, 0)
                x_bias(1)

            def stage_y(g, more):
                x1_power(g, TILES - 1)
                if more:
                    k_diagonal(g + 1, 0)
                    k_diagonal(g + 1, 1)
                    x_bias(g + 1)
                    subtract_max(g + 1, 0)

            pool.wait_ge(consts_ready, 1)
            x_power(0)
            w_split_lo(0)
            w_split_lo(1)
            pool.wait_ge(rows_loaded, 16)
            x_bias(0)
            pool.wait_ge(heads_ready, 1)
            k_diagonal(0, 1)
            w_split_lo(2)
            k_diagonal(0, 2)
            k_diagonal(0, 3)
            subtract_max(0, 1)
            first_group()
            with pool.Fori(1, GROUPS - 1) as g:
                stage_x(g, g - 1, True)
                stage_y(g, True)
            last = GROUPS - 1
            stage_x(last, last - 1, False)
            stage_y(last, False)
            for t in range(TILES):
                y_bias(last, t)

        @block.vector
        def _(dve):
            dve.memset(v_diag[:], 0.0).then_inc(mask_step, 1)
            dve.wait_ge(ident_ready, 2)
            dve.wait_ge(mask_step, 1)

            def masks():
                dve.wait_ge(mask_loaded, 16 * BT)
                dve.tensor_scalar(mask_add[:], mask_raw, 0, None, ALU.is_equal).then_inc(mask_step, 1)
                dve.wait_ge(mask_step, 2)
                dve.tensor_reduce(all_masked[:], mask_add[:], AX_X, ALU.min).then_inc(mask_step, 1)
                dve.wait_ge(mask_step, 3)
                dve.tensor_scalar(score_mul[:], all_masked[:], -SCALE, SCALE, ALU.mult, ALU.add)\
                    .then_inc(mask_step, 1)
                dve.tensor_tensor(mask_add[:], mask_add[:], all_masked[:].unsqueeze(2).broadcast_to([P, NT, SEQ]),
                                  ALU.subtract).then_inc(mask_step, 1)
                dve.wait_ge(mask_step, 5)
                dve.tensor_scalar(mask_add[:], mask_add[:], MASKED, None, ALU.mult).then_inc(mask_step, 1)
                dve.wait_ge(mask_step, 6)

            def w_split_lo(s):
                dve.wait_ge(w_hi_done, s + 1)
                cols = slice(s * WCH, (s + 1) * WCH)
                dve.tensor_tensor(w_lo[:, cols], w_raw[:, s % 2, :], w_hi[:, cols].bitcast(F32), ALU.subtract)\
                    .then_inc(w_lo_dve, 1)

            def cond_silu_():
                dve.wait_ge(cond_tanh_done, 1)
                dve.scalar_tensor_tensor(out=cond[:], in0=cond_tanh[:], scalar=1.0, in1=cond[:], op0=ALU.add,
                                         op1=ALU.mult).then_inc(mod_step, 1)
                dve.wait_ge(mod_step, 1)
                dve.tensor_scalar(cond[:], cond[:], 0.5, None, ALU.mult).then_inc(cond_silu, 1)

            def modulation():
                dve.wait_ge(vec_loaded, 16)
                dve.wait_ge(mod_done, 2)
                for m in range(CK):
                    cols = slice(m * BATCH, (m + 1) * BATCH)
                    dve.tensor_scalar(scale_w[:, m, :], ps_m[:, 0, cols], vec[:, SCALE_B + m:SCALE_B + m + 1], 1.0,
                                      ALU.add, ALU.add).then_inc(mod_step, 1)
                    dve.tensor_scalar(shift[:, m, :], ps_m[:, 1, cols], vec[:, SHIFT_B + m:SHIFT_B + m + 1], None,
                                      ALU.add).then_inc(mod_step, 1)
                dve.wait_ge(mod_step, 2 * CK + 1)
                dve.tensor_scalar(scale_w[:], scale_w[:], 0.1, 10.0, ALU.max, ALU.min).then_inc(mod_step, 1)
                dve.wait_ge(mod_step, 2 * CK + 2)
                for m in range(CK):
                    dve.tensor_scalar(scale_w[:, m, :], scale_w[:, m, :], vec[:, NORM_W + m:NORM_W + m + 1], None,
                                      ALU.mult).then_inc(ps_m_read if m == 0 else mod_step, 1)
                dve.wait_ge(ps_m_read, 1)
                dve.wait_ge(mod_step, 3 * CK + 1)

            def by_seq(table, g, c):
                return table[:, c, bass.ds(BG * g, BG)].unsqueeze(2).broadcast_to([P, BG, SEQ])

            def adaln(g, src, src_done, scaled, full):
                seqs = lambda ap: ap.rearrange("p (b k) -> p b k", b=BG)
                for c in range(CK):
                    dve.wait_ge(src_done, CK * g + c + 1)
                    dve.tensor_tensor(seqs(h_full[:, c, :]), seqs(src[:, c, :]), by_seq(scale_w, g, c), ALU.mult)\
                        .then_inc(scaled, 1)
                for c in range(CK):
                    dve.wait_ge(scaled, CK * g + c + 1)
                    dve.tensor_tensor(seqs(h_full[:, c, :]), seqs(h_full[:, c, :]), by_seq(shift, g, c), ALU.add)\
                        .then_inc(full, 1)

            def adaln_second(g, hi, hi_done, lo, lo_done):
                for c in range(CK):
                    dve.wait_ge(hi_done, CK * g + c + 1)
                    dve.tensor_tensor(lo[:, c, :], h_full[:, c, :], hi[:, c, :].bitcast(F32), ALU.subtract)\
                        .then_inc(lo_done, 1)

            def adaln1(g, bank=ps_p):
                if isinstance(g, int) and g < 2:
                    pass
                else:
                    dve.wait_ge(h2_lo_done, CK * (g - 1))
                adaln(g, bank, xt_done, h1_scaled, h1_full)

            def h1_second(g):
                adaln_second(g, h1_hi, h1_hi_done, h1_lo, h1_lo_done)

            def adaln2(g, more):
                if more:
                    dve.wait_ge(h1_lo_done, CK * (g + 2))
                adaln(g, ps_c, x1t_done, h2_scaled, h2_full)

            def h2_second(g):
                adaln_second(g, h2_hi, h2_hi_done, h2_lo, h2_lo_done)

            flat = lambda i: v_part[:, i].rearrange("p j h d -> p (j h d)")

            def v_second(g, t):
                n = TILES * g + t
                dve.wait_ge(v1_done, n + 1)
                if not is0(n):
                    dve.wait_ge(v3_done, n)
                dve.tensor_tensor(v_rest[:], v_bank(g, t), flat(0), ALU.subtract).then_inc(v_rest_done, 1)

            def v_third(g, t):
                n = TILES * g + t
                dve.wait_ge(v_rest_done, n + 1)
                dve.tensor_copy(flat(1), v_rest[:]).then_inc(v2_done, 1)
                dve.wait_ge(v2_done, n + 1)
                dve.tensor_tensor(flat(2), v_rest[:], flat(1), ALU.subtract).then_inc(v3_done, 1)

            heads = lambda ap: ap.rearrange("p (h k) -> p h k", k=SEQ)

            def scores_masked(g, t):
                n = TILES * g + t
                if isinstance(n, int) and n < 2:
                    pass
                else:
                    dve.wait_ge(pt_done, 2 * n - 2)
                for c in range(CK):
                    dve.wait_ge(s_done, 2 * n + c + 1)
                    dve.scalar_tensor_tensor(out=heads(s_sb[:, t % 2, c * 512:(c + 1) * 512]),
                                             in0=heads(ps_s[:, c, :]), scalar=score_mul[:, bass.ds(n, 1)],
                                             in1=mask_add[:, bass.ds(n, 1), :].broadcast_to([P, HC, SEQ]),
                                             op0=ALU.mult, op1=ALU.add).then_inc(s_masked, 1)

            def scores_max(g, t):
                n = TILES * g + t
                dve.wait_ge(s_masked, 2 * n + 2)
                dve.tensor_reduce(s_max[:, t % 2, :], heads(s_sb[:, t % 2, :]), AX_X, ALU.max).then_inc(max_done, 1)

            def p_second(g, t):
                n = TILES * g + t
                if not is0(n):
                    dve.wait_ge(pv_done, n)
                for half in range(2):
                    dve.wait_ge(p_hi_done, 2 * n + half + 1)
                    js = slice(half * 4, half * 4 + 4)
                    dve.tensor_tensor(p_lo[:, js, :].rearrange("p j q -> p (j q)"), ps_p[:, half, :],
                                      p_hi[:, js, :].rearrange("p j q -> p (j q)"), ALU.subtract)\
                        .then_inc(p_lo_done, 1)

            def normalise_o(g, t):
                n = TILES * g + t
                dve.wait_ge(pv_done, n + 1)
                if not is0(n):
                    dve.wait_ge(ot_done, n)
                pv = [ps_c[b * SEQ:(b + 1) * SEQ, :, b * HC * VW:(b + 1) * HC * VW]
                      .rearrange("p c (h d) -> p c h d", d=VW) for b in range(BT)]
                for b in range(BT):
                    dve.reciprocal(sum_inv[b * SEQ:(b + 1) * SEQ], pv[b][:, :, :, D]).then_inc(sum_inverted, 1)
                for b in range(BT):
                    dve.wait_ge(sum_inverted, 2 * n + b + 1)
                    rows_ = slice(b * SEQ, (b + 1) * SEQ)
                    dve.tensor_tensor(o_sb[rows_, :].rearrange("p (c h d) -> p c h d", c=CK, h=HC), pv[b][:, :, :, 0:D],
                                      sum_inv[rows_].unsqueeze(3).broadcast_to([SEQ, CK, HC, D]), ALU.mult)\
                        .then_inc(o_done, 1)

            def o_second(g, t):
                n = TILES * g + t
                dve.wait_ge(o_hi_done, n + 1)
                dve.tensor_tensor(o_lo[:], ps_c[:, 0, 0:C], o_hi[:].bitcast(F32), ALU.subtract)\
                    .then_inc(o_lo_done, 1)

            def x1_add(g, t):
                n = TILES * g + t
                dve.wait_ge(proj_done, n + 1)
                dve.wait_ge(x_biased, n + 1)
                if not is0(g):
                    dve.wait_ge(y_biased, n - TILES + 1)
                dve.tensor_tensor(x1[:, t, :], ps_c[:, 1, 0:C], x_res[:, t, :], ALU.add).then_inc(x1_done, 1)

            def x_clamp(g):
                if not is0(g):
                    dve.wait_ge(x_normed, TILES * g)
                dve.wait_ge(x_powed, g + 1)
                dve.tensor_scalar(x_inv[:], x_pow[:], 1.0 / EPS, None, ALU.min).then_inc(x_inverted, 1)

            def x1_clamp(g, t):
                n = TILES * g + t
                if not is0(g):
                    dve.wait_ge(x1_normed, n - TILES + 1)
                dve.wait_ge(x1_powed, n + 1)
                dve.tensor_scalar(x1_inv[:, t:t + 1], x1_pow[:, t:t + 1], 1.0 / EPS, None, ALU.min)\
                    .then_inc(x1_inverted, 1)

            def gate_up(m, j, bank=ps_m):
                n = FJ * m + j
                dve.wait_ge(up_done, n + 1)
                dve.wait_ge(gate_read, n + 1)
                dve.scalar_tensor_tensor(out=gate[:, j % 2, :], in0=bank[:, 1, :],
                                         scalar=vec[:, MLP_B1 + FJ + j:MLP_B1 + FJ + j + 1], in1=gate[:, j % 2, :],
                                         op0=ALU.add, op1=ALU.mult).then_inc(up_read, 1)

            def gated(m, j):
                n = FJ * m + j
                dve.wait_ge(up_read, n + 1)
                dve.scalar_tensor_tensor(out=gate[:, j % 2, :], in0=gate_tanh[:, j % 2, :], scalar=1.0,
                                         in1=gate[:, j % 2, :], op0=ALU.add, op1=ALU.mult).then_inc(g_done, 1)

            def g_second(m, j):
                dve.wait_ge(g_hi_done, FJ * m + j + 1)
                dve.tensor_tensor(g_lo[:, j, :], gate[:, j % 2, :], g_hi[:, j, :].bitcast(F32), ALU.subtract)\
                    .then_inc((g_lo_even, g_lo_odd)[j % 2], 1)

            def y_add(m, t, bank=None):
                n = TILES * m + t
                dve.wait_ge(down_done, n + 1)
                dve.wait_ge(y_biased, n + 1)
                dve.tensor_tensor(y[:, t, :], ps_m[:, t % 2, 0:C] if bank is None else bank, y[:, t, :], ALU.add).then_inc(ps_m_read, 1)

            def stage_x(g, m, more):
                for t in range(TILES):
                    if 0 < t < TILES - 1:
                        v_second(g, t + 1)
                        scores_masked(g, t + 1)
                    if t > 0:
                        x1_add(g, t - 1)
                    if 0 < t < TILES - 1:
                        scores_max(g, t + 1)
                    if t + 1 < TILES:
                        v_third(g, t + 1)
                    if more and t == 2:
                        x_clamp(g + 1)
                    p_second(g, t)
                    gate_up(m, 2 * t)
                    if t < TILES - 1:
                        gated(m, 2 * t)
                    normalise_o(g, t)
                    if t == 3:
                        gated(m, 2 * t)
                    if t > 0:
                        x1_clamp(g, t - 1)
                    gate_up(m, 2 * t + 1)
                    o_second(g, t)
                    gated(m, 2 * t + 1)
                    g_second(m, 2 * t)

            def first_group():
                p_second(0, 0)
                scores_max(0, 1)
                normalise_o(0, 0)
                v_second(0, 2)
                v_third(0, 2)
                scores_masked(0, 2)
                o_second(0, 0)

                p_second(0, 1)
                x1_add(0, 0)
                x_clamp(1)
                scores_max(0, 2)
                normalise_o(0, 1)
                v_second(0, 3)
                v_third(0, 3)
                scores_masked(0, 3)
                o_second(0, 1)
                x1_clamp(0, 0)

                p_second(0, 2)
                x1_add(0, 1)
                scores_max(0, 3)
                normalise_o(0, 2)
                adaln1(1, ps_m)
                o_second(0, 2)
                x1_clamp(0, 1)

                p_second(0, 3)
                x1_add(0, 2)
                h1_second(1)
                normalise_o(0, 3)
                o_second(0, 3)
                x1_clamp(0, 2)
                v_second(1, 0)
                v_third(1, 0)
                x1_add(0, 3)
                w_split_lo(7)
                x1_clamp(0, 3)
                adaln2(0, True)
                scores_masked(1, 0)
                scores_max(1, 0)
                h2_second(0)
                v_second(1, 1)
                scores_masked(1, 1)
                scores_max(1, 1)

            def stage_y(g, m, more):
                x1_add(g, TILES - 1)
                if more:
                    adaln1(g + 1)
                    h1_second(g + 1)
                x1_clamp(g, TILES - 1)
                y_add(m, 0)
                if more:
                    y_add(m, 1)
                adaln2(g, more)
                if not more:
                    y_add(m, 1)
                h2_second(g)
                y_add(m, 2)
                if more:
                    v_second(g + 1, 0)
                    v_third(g + 1, 0)
                    scores_masked(g + 1, 0)
                    scores_max(g + 1, 0)
                y_add(m, 3)
                if more:
                    scores_masked(g + 1, 1)
                    v_second(g + 1, 1)
                    scores_max(g + 1, 1)

            cond_silu_()
            dve.tensor_reduce(head_rows[:], ident[:].rearrange("p (h d) -> p h d", d=D), AX_X, ALU.add)\
                .then_inc(heads_ready, 1)
            for hp in range(2):
                for b in range(BT):
                    last = dve.memset(v_diag[hp * SEQ:(hp + 1) * SEQ, :, :, 0, b, hp, D], 1.0)
            last.then_inc(vdiag_ready, 1)
            x_clamp(0)
            modulation()
            adaln1(0)
            h1_second(0)
            masks()
            dve.wait_ge(heads_ready, 1)
            for c in range(CK):
                dve.wait_ge(k_copied, c + 1)
                dve.tensor_tensor(k_diag[:, 0, c].rearrange("p b (h k) -> p b h k", h=HC),
                                  k_t[:, c, 0:P].rearrange("p (b k) -> p b k", b=BT).unsqueeze(2)
                                  .broadcast_to([P, BT, HC, SEQ]),
                                  head_rows[:].unsqueeze(1).unsqueeze(3).broadcast_to([P, BT, HC, SEQ]), ALU.mult)\
                    .then_inc(kdiag_first, 1)
            v_second(0, 0)
            v_third(0, 0)
            dve.tensor_scalar(half_b1[:], vec[:, MLP_B1:MLP_B1 + FJ], 0.5, None, ALU.mult).then_inc(half_b1_ready, 1)
            scores_masked(0, 0)
            scores_max(0, 0)
            dve.wait_ge(max_done, 1)
            dve.tensor_tensor(heads(s_sb[:, 0, :]), heads(s_sb[:, 0, :]),
                              s_max[:, 0, :].unsqueeze(2).broadcast_to([P, HEADS, SEQ]), ALU.subtract)\
                .then_inc(max_subtracted, 1)
            v_second(0, 1)
            scores_masked(0, 1)
            v_third(0, 1)
            first_group()
            with dve.Fori(1, GROUPS - 1) as g:
                stage_x(g, g - 1, True)
                stage_y(g, g - 1, True)
            last = GROUPS - 1
            stage_x(last, last - 1, False)
            stage_y(last, last - 1, False)
            for j in range(FJ):
                gate_up(last, j, (ps_s, ps_m)[j % 2])
                gated(last, j)
                g_second(last, j)
            for t in range(TILES):
                y_add(last, t, last_banks[t])


def kernel(x, cond_1024, mask_BxS_ik0, L0_cond_norm_w, L0_cond_scale_w, L0_cond_scale_b, L0_cond_shift_w,
           L0_cond_shift_b, L0_cond_qkv_w, L0_cond_proj_w, L0_cond_proj_b, L0_cond_mlp_w1, L0_cond_mlp_b1,
           L0_cond_mlp_w2, L0_cond_mlp_b2):
    import numpy as np
    import concourse.bacc as bacc
    from concourse.bass_utils import run_bass_kernel_spmd

    def by_input(w):
        w = np.asarray(w)
        return w.T.reshape(-1, P, w.shape[0]).transpose(1, 0, 2).reshape(P, -1)

    def columns(v):
        return np.asarray(v).reshape(-1, P).T

    qkv = np.asarray(L0_cond_qkv_w)
    arrays = {
        "x": np.asarray(x).reshape(BATCH * SEQ, C),
        "cond_t": np.asarray(cond_1024).T.reshape(CK, P, BATCH).transpose(1, 0, 2),
        "mask": np.asarray(mask_BxS_ik0),
        "weights": np.concatenate([by_input(qkv[:2 * C]), by_input(qkv[2 * C:]), by_input(L0_cond_proj_w),
                                   by_input(L0_cond_mlp_w1), by_input(L0_cond_mlp_w2)], axis=1),
        "mod_w": np.stack([by_input(L0_cond_scale_w), by_input(L0_cond_shift_w)], axis=1).reshape(P, 2, CK, C),
        "vecs": np.concatenate([columns(v) for v in (L0_cond_scale_b, L0_cond_shift_b, L0_cond_norm_w,
                                                     L0_cond_mlp_b1)], axis=1),
        "rows": np.stack([np.asarray(L0_cond_proj_b), np.asarray(L0_cond_mlp_b2)]),
    }
    nc = bacc.Bacc("TRN2", target_bir_lowering=False, num_devices=1)
    args = {}
    for name, a in arrays.items():
        arrays[name] = np.ascontiguousarray(a)
        args[name] = nc.dram_tensor(name, a.shape, mybir.dt.from_np(a.dtype), kind="ExternalInput").ap()
    args["out"] = nc.dram_tensor("out", (BATCH * SEQ, C), F32, kind="ExternalOutput").ap()
    block_kernel(nc, **args)
    r = run_bass_kernel_spmd(nc, [arrays], core_ids=[0])
    return r.results[0]["out"].reshape(BATCH, SEQ, C)
```
